# Optimizing a Trainium2 kernel written in Bass

```python
import numpy as np
import jax
import jax.numpy as jnp

def _softmax(x, axis=-1):
    return jax.nn.softmax(x, axis=axis)

def _gelu(x):
    return jax.nn.gelu(x, approximate=True)

def _silu(x):
    return jax.nn.silu(x)

def _sigmoid(x):
    return jax.nn.sigmoid(x)

def _layernorm(x, axis=-1, eps=1e-05):
    m = jnp.mean(x, axis=axis, keepdims=True)
    v = jnp.var(x, axis=axis, keepdims=True)
    return (x - m) / jnp.sqrt(v + eps)

def _scatter_add(tgt, idx, src, axis=0):
    return tgt.at[idx].add(src)

def _segment_sum(src, seg, n):
    return jax.ops.segment_sum(src, seg, n)
kernel_name = 'mk_dlrm_tower_d1_rec_r8_d2883c'

def setup_inputs(seed: int=0):
    np.random.seed(seed)
    _w = jnp.asarray

    def _rec_inputs():
        import jax
        import jax.numpy as jnp
        _tk = jax.random.key(seed)
        dense_ctx = jax.random.normal(jax.random.fold_in(_tk, 190), (1024, 16), jnp.float32)
        ids = jnp.stack([jax.random.randint(jax.random.fold_in(_tk, 200 + f), (1024,), 0, v, jnp.int32) for f, v in enumerate([12500, 1000, 1250, 12500, 125000, 1000, 1000, 12500, 1250, 12500, 1000, 12500, 1250, 1250, 1000, 1000, 1000, 1000, 125000, 12500, 125000, 1000, 12500, 12500, 1250, 125000, 12500, 125000, 125000, 12500, 1250, 125000, 1250, 1250, 1000, 1000, 12500, 1250, 1000])], axis=1)
        tbl_0 = 0.05 * jax.random.normal(jax.random.fold_in(_tk, 500 + 0), (12500, 16), jnp.float32)
        tbl_1 = 0.05 * jax.random.normal(jax.random.fold_in(_tk, 500 + 1), (1000, 16), jnp.float32)
        tbl_2 = 0.05 * jax.random.normal(jax.random.fold_in(_tk, 500 + 2), (1250, 16), jnp.float32)
        tbl_3 = 0.05 * jax.random.normal(jax.random.fold_in(_tk, 500 + 3), (12500, 16), jnp.float32)
        tbl_4 = 0.05 * jax.random.normal(jax.random.fold_in(_tk, 500 + 4), (125000, 16), jnp.float32)
        tbl_5 = 0.05 * jax.random.normal(jax.random.fold_in(_tk, 500 + 5), (1000, 16), jnp.float32)
        tbl_6 = 0.05 * jax.random.normal(jax.random.fold_in(_tk, 500 + 6), (1000, 16), jnp.float32)
        tbl_7 = 0.05 * jax.random.normal(jax.random.fold_in(_tk, 500 + 7), (12500, 16), jnp.float32)
        tbl_8 = 0.05 * jax.random.normal(jax.random.fold_in(_tk, 500 + 8), (1250, 16), jnp.float32)
        tbl_9 = 0.05 * jax.random.normal(jax.random.fold_in(_tk, 500 + 9), (12500, 16), jnp.float32)
        tbl_10 = 0.05 * jax.random.normal(jax.random.fold_in(_tk, 500 + 10), (1000, 16), jnp.float32)
        tbl_11 = 0.05 * jax.random.normal(jax.random.fold_in(_tk, 500 + 11), (12500, 16), jnp.float32)
        tbl_12 = 0.05 * jax.random.normal(jax.random.fold_in(_tk, 500 + 12), (1250, 16), jnp.float32)
        tbl_13 = 0.05 * jax.random.normal(jax.random.fold_in(_tk, 500 + 13), (1250, 16), jnp.float32)
        tbl_14 = 0.05 * jax.random.normal(jax.random.fold_in(_tk, 500 + 14), (1000, 16), jnp.float32)
        tbl_15 = 0.05 * jax.random.normal(jax.random.fold_in(_tk, 500 + 15), (1000, 16), jnp.float32)
        tbl_16 = 0.05 * jax.random.normal(jax.random.fold_in(_tk, 500 + 16), (1000, 16), jnp.float32)
        tbl_17 = 0.05 * jax.random.normal(jax.random.fold_in(_tk, 500 + 17), (1000, 16), jnp.float32)
        tbl_18 = 0.05 * jax.random.normal(jax.random.fold_in(_tk, 500 + 18), (125000, 16), jnp.float32)
        tbl_19 = 0.05 * jax.random.normal(jax.random.fold_in(_tk, 500 + 19), (12500, 16), jnp.float32)
        tbl_20 = 0.05 * jax.random.normal(jax.random.fold_in(_tk, 500 + 20), (125000, 16), jnp.float32)
        tbl_21 = 0.05 * jax.random.normal(jax.random.fold_in(_tk, 500 + 21), (1000, 16), jnp.float32)
        tbl_22 = 0.05 * jax.random.normal(jax.random.fold_in(_tk, 500 + 22), (12500, 16), jnp.float32)
        tbl_23 = 0.05 * jax.random.normal(jax.random.fold_in(_tk, 500 + 23), (12500, 16), jnp.float32)
        tbl_24 = 0.05 * jax.random.normal(jax.random.fold_in(_tk, 500 + 24), (1250, 16), jnp.float32)
        tbl_25 = 0.05 * jax.random.normal(jax.random.fold_in(_tk, 500 + 25), (125000, 16), jnp.float32)
        tbl_26 = 0.05 * jax.random.normal(jax.random.fold_in(_tk, 500 + 26), (12500, 16), jnp.float32)
        tbl_27 = 0.05 * jax.random.normal(jax.random.fold_in(_tk, 500 + 27), (125000, 16), jnp.float32)
        tbl_28 = 0.05 * jax.random.normal(jax.random.fold_in(_tk, 500 + 28), (125000, 16), jnp.float32)
        tbl_29 = 0.05 * jax.random.normal(jax.random.fold_in(_tk, 500 + 29), (12500, 16), jnp.float32)
        tbl_30 = 0.05 * jax.random.normal(jax.random.fold_in(_tk, 500 + 30), (1250, 16), jnp.float32)
        tbl_31 = 0.05 * jax.random.normal(jax.random.fold_in(_tk, 500 + 31), (125000, 16), jnp.float32)
        tbl_32 = 0.05 * jax.random.normal(jax.random.fold_in(_tk, 500 + 32), (1250, 16), jnp.float32)
        tbl_33 = 0.05 * jax.random.normal(jax.random.fold_in(_tk, 500 + 33), (1250, 16), jnp.float32)
        tbl_34 = 0.05 * jax.random.normal(jax.random.fold_in(_tk, 500 + 34), (1000, 16), jnp.float32)
        tbl_35 = 0.05 * jax.random.normal(jax.random.fold_in(_tk, 500 + 35), (1000, 16), jnp.float32)
        tbl_36 = 0.05 * jax.random.normal(jax.random.fold_in(_tk, 500 + 36), (12500, 16), jnp.float32)
        tbl_37 = 0.05 * jax.random.normal(jax.random.fold_in(_tk, 500 + 37), (1250, 16), jnp.float32)
        tbl_38 = 0.05 * jax.random.normal(jax.random.fold_in(_tk, 500 + 38), (1000, 16), jnp.float32)
        _rk = jax.random.fold_in(_tk, 7)
        W_top1 = 0.0606339 * jax.random.normal(jax.random.fold_in(_tk, 801), (272, 512), jnp.float32)
        W_top2 = 0.0441942 * jax.random.normal(jax.random.fold_in(_tk, 802), (512, 256), jnp.float32)
        W_top3 = 0.0625 * jax.random.normal(jax.random.fold_in(_tk, 803), (256, 1), jnp.float32)
        b_top1 = jnp.zeros((512,), jnp.float32)
        b_top2 = jnp.zeros((256,), jnp.float32)
        return (dense_ctx, ids, tbl_0, tbl_1, tbl_2, tbl_3, tbl_4, tbl_5, tbl_6, tbl_7, tbl_8, tbl_9, tbl_10, tbl_11, tbl_12, tbl_13, tbl_14, tbl_15, tbl_16, tbl_17, tbl_18, tbl_19, tbl_20, tbl_21, tbl_22, tbl_23, tbl_24, tbl_25, tbl_26, tbl_27, tbl_28, tbl_29, tbl_30, tbl_31, tbl_32, tbl_33, tbl_34, tbl_35, tbl_36, tbl_37, tbl_38, W_top1, b_top1, W_top2, b_top2, W_top3)
    dense_ctx, ids, tbl_0, tbl_1, tbl_2, tbl_3, tbl_4, tbl_5, tbl_6, tbl_7, tbl_8, tbl_9, tbl_10, tbl_11, tbl_12, tbl_13, tbl_14, tbl_15, tbl_16, tbl_17, tbl_18, tbl_19, tbl_20, tbl_21, tbl_22, tbl_23, tbl_24, tbl_25, tbl_26, tbl_27, tbl_28, tbl_29, tbl_30, tbl_31, tbl_32, tbl_33, tbl_34, tbl_35, tbl_36, tbl_37, tbl_38, W_top1, b_top1, W_top2, b_top2, W_top3 = _rec_inputs()

    def _L0_rec_setup():
        import jax, jax.numpy as jnp
        import numpy as np
        F0 = 39
        CIN_SIZES = [128, 128, 128]
        B, D = (512, 16)

        def _cin_forward(x, weights, biases):
            x0 = x
            xk = x
            fields = [F0] + CIN_SIZES
            outs = []
            for idx, s in enumerate(CIN_SIZES):
                fk = fields[idx]
                w = weights[idx].reshape(F0, fk, s)
                out = jnp.einsum('bid,bjd,ijs->bsd', x0, xk, w) + biases[idx][None, :, None]
                outs.append(out)
                xk = out
            res = jnp.concatenate(outs[1:], axis=1)
            return jnp.sum(res, axis=-1)
        key = jax.random.key(seed)
        ks = jax.random.split(key, 7)
        fields = [F0] + CIN_SIZES
        inp = {'x': jax.random.normal(ks[0], (B, F0, D), dtype=jnp.float32)}
        for i, s in enumerate(CIN_SIZES):
            m = fields[i] * F0
            inp[f'w{i}'] = jax.random.normal(ks[1 + 2 * i], (m, s), dtype=jnp.float32) * (2.0 / (m + s)) ** 0.5
            inp[f'b{i}'] = jax.random.normal(ks[2 + 2 * i], (s,), dtype=jnp.float32) * 0.02
        return inp
    _L0_rec_all = _L0_rec_setup()
    _L0_rec_in = {k: v for k, v in _L0_rec_all.items() if k in ('w0', 'b0', 'w1', 'b1', 'w2', 'b2')}
    del _L0_rec_all
    return {'dense_ctx': dense_ctx, 'ids': ids, 'tbl_0': tbl_0, 'tbl_1': tbl_1, 'tbl_2': tbl_2, 'tbl_3': tbl_3, 'tbl_4': tbl_4, 'tbl_5': tbl_5, 'tbl_6': tbl_6, 'tbl_7': tbl_7, 'tbl_8': tbl_8, 'tbl_9': tbl_9, 'tbl_10': tbl_10, 'tbl_11': tbl_11, 'tbl_12': tbl_12, 'tbl_13': tbl_13, 'tbl_14': tbl_14, 'tbl_15': tbl_15, 'tbl_16': tbl_16, 'tbl_17': tbl_17, 'tbl_18': tbl_18, 'tbl_19': tbl_19, 'tbl_20': tbl_20, 'tbl_21': tbl_21, 'tbl_22': tbl_22, 'tbl_23': tbl_23, 'tbl_24': tbl_24, 'tbl_25': tbl_25, 'tbl_26': tbl_26, 'tbl_27': tbl_27, 'tbl_28': tbl_28, 'tbl_29': tbl_29, 'tbl_30': tbl_30, 'tbl_31': tbl_31, 'tbl_32': tbl_32, 'tbl_33': tbl_33, 'tbl_34': tbl_34, 'tbl_35': tbl_35, 'tbl_36': tbl_36, 'tbl_37': tbl_37, 'tbl_38': tbl_38, 'W_top1': W_top1, 'b_top1': b_top1, 'W_top2': W_top2, 'b_top2': b_top2, 'W_top3': W_top3, 'L0_rec_w0': _L0_rec_in['w0'], 'L0_rec_b0': _L0_rec_in['b0'], 'L0_rec_w1': _L0_rec_in['w1'], 'L0_rec_b1': _L0_rec_in['b1'], 'L0_rec_w2': _L0_rec_in['w2'], 'L0_rec_b2': _L0_rec_in['b2']}

def reference(dense_ctx, ids, tbl_0, tbl_1, tbl_2, tbl_3, tbl_4, tbl_5, tbl_6, tbl_7, tbl_8, tbl_9, tbl_10, tbl_11, tbl_12, tbl_13, tbl_14, tbl_15, tbl_16, tbl_17, tbl_18, tbl_19, tbl_20, tbl_21, tbl_22, tbl_23, tbl_24, tbl_25, tbl_26, tbl_27, tbl_28, tbl_29, tbl_30, tbl_31, tbl_32, tbl_33, tbl_34, tbl_35, tbl_36, tbl_37, tbl_38, W_top1, b_top1, W_top2, b_top2, W_top3, L0_rec_w0, L0_rec_b0, L0_rec_w1, L0_rec_b1, L0_rec_w2, L0_rec_b2):
    import jax
    import jax.numpy as jnp

    def _L0_rec_ref(x, w0, b0, w1, b1, w2, b2):
        import jax, jax.numpy as jnp
        import numpy as np
        F0 = 39
        CIN_SIZES = [128, 128, 128]
        B, D = (512, 16)

        def _cin_forward(x, weights, biases):
            x0 = x
            xk = x
            fields = [F0] + CIN_SIZES
            outs = []
            for idx, s in enumerate(CIN_SIZES):
                fk = fields[idx]
                w = weights[idx].reshape(F0, fk, s)
                out = jnp.einsum('bid,bjd,ijs->bsd', x0, xk, w) + biases[idx][None, :, None]
                outs.append(out)
                xk = out
            res = jnp.concatenate(outs[1:], axis=1)
            return jnp.sum(res, axis=-1)
        return _cin_forward(x, [w0, w1, w2], [b0, b1, b2])
    e = jnp.stack([tbl_0[ids[:, 0]], tbl_1[ids[:, 1]], tbl_2[ids[:, 2]], tbl_3[ids[:, 3]], tbl_4[ids[:, 4]], tbl_5[ids[:, 5]], tbl_6[ids[:, 6]], tbl_7[ids[:, 7]], tbl_8[ids[:, 8]], tbl_9[ids[:, 9]], tbl_10[ids[:, 10]], tbl_11[ids[:, 11]], tbl_12[ids[:, 12]], tbl_13[ids[:, 13]], tbl_14[ids[:, 14]], tbl_15[ids[:, 15]], tbl_16[ids[:, 16]], tbl_17[ids[:, 17]], tbl_18[ids[:, 18]], tbl_19[ids[:, 19]], tbl_20[ids[:, 20]], tbl_21[ids[:, 21]], tbl_22[ids[:, 22]], tbl_23[ids[:, 23]], tbl_24[ids[:, 24]], tbl_25[ids[:, 25]], tbl_26[ids[:, 26]], tbl_27[ids[:, 27]], tbl_28[ids[:, 28]], tbl_29[ids[:, 29]], tbl_30[ids[:, 30]], tbl_31[ids[:, 31]], tbl_32[ids[:, 32]], tbl_33[ids[:, 33]], tbl_34[ids[:, 34]], tbl_35[ids[:, 35]], tbl_36[ids[:, 36]], tbl_37[ids[:, 37]], tbl_38[ids[:, 38]]], axis=1)
    z = _L0_rec_ref(e, L0_rec_w0, L0_rec_b0, L0_rec_w1, L0_rec_b1, L0_rec_w2, L0_rec_b2)
    z = z.reshape(z.shape[0], -1)
    h = jnp.concatenate([z, dense_ctx], axis=1)
    h = jnp.maximum(h @ W_top1 + b_top1, 0.0)
    h = jnp.maximum(h @ W_top2 + b_top2, 0.0)
    y = h @ W_top3
    return y

_drawn_inputs = setup_inputs


def setup_inputs(seed=0):
    import zlib

    import numpy as np

    out = dict(_drawn_inputs(seed))
    spreads = {'b_top1': (0.0, 0.8), 'b_top2': (0.0, 0.648)}
    factors = {'tbl_0': 8.0,
     'tbl_1': 8.0,
     'tbl_2': 8.0,
     'tbl_3': 8.0,
     'tbl_4': 8.0,
     'tbl_5': 8.0,
     'tbl_6': 8.0,
     'tbl_7': 8.0,
     'tbl_8': 8.0,
     'tbl_9': 8.0,
     'tbl_10': 8.0,
     'tbl_11': 8.0,
     'tbl_12': 8.0,
     'tbl_13': 8.0,
     'tbl_14': 8.0,
     'tbl_15': 8.0,
     'tbl_16': 8.0,
     'tbl_17': 8.0,
     'tbl_18': 8.0,
     'tbl_19': 8.0,
     'tbl_20': 8.0,
     'tbl_21': 8.0,
     'tbl_22': 8.0,
     'tbl_23': 8.0,
     'tbl_24': 8.0,
     'tbl_25': 8.0,
     'tbl_26': 8.0,
     'tbl_27': 8.0,
     'tbl_28': 8.0,
     'tbl_29': 8.0,
     'tbl_30': 8.0,
     'tbl_31': 8.0,
     'tbl_32': 8.0,
     'tbl_33': 8.0,
     'tbl_34': 8.0,
     'tbl_35': 8.0,
     'tbl_36': 8.0,
     'tbl_37': 8.0,
     'tbl_38': 8.0,
     'L0_rec_w0': 8.0,
     'L0_rec_b0': 3.409,
     'L0_rec_w1': 3.462,
     'L0_rec_w2': 2.826,
     'dense_ctx': 3.158,
     'L0_rec_b1': 3.548,
     'L0_rec_b2': 3.955}
    for name, (base, spread) in spreads.items():
        noise = np.random.default_rng([zlib.crc32(name.encode()), seed]).standard_normal(out[name].shape)
        drawn = base * np.exp(spread * noise) if base else spread * noise
        out[name] = jnp.asarray(drawn.astype(out[name].dtype))
    for name, factor in factors.items():
        out[name] = (out[name] * factor).astype(out[name].dtype)
    return out
```

```python
from contextlib import ExitStack

import concourse.bass as bass
from concourse import mybir

FIELDS, DIM, BATCH, MAPS = 39, 16, 1024, 128
PART = 128
TILES_G = 4
GROUPS_B = 4
TILES_B = TILES_G * GROUPS_B
BLOCKS = BATCH // PART
BATCH_T = PART // DIM
GROUP_N = TILES_G * PART
BLOCK_N = PART * DIM
DELTAS = FIELDS // 2 + 1
SHIFTS = 3
ROWS = SHIFTS * FIELDS
PAIR_K = -(-DELTAS // SHIFTS)
PER = 4
CHUNKS = -(-FIELDS // PER)
BANKS = 4
ACT_CHUNKS = (1, 4, 7)
ACT_FIELDS = PER * len(ACT_CHUNKS)
DVE_FIELDS = FIELDS - ACT_FIELDS
COLS = FIELDS + 1
LAG = 2
SLOTS_G = TILES_G * CHUNKS
HIDDEN1, HIDDEN2 = 512, 256
Z_FIRST, Z_SLOTS, Z_PER = 17, 8, 5
PREP_SLOTS = (104, 110)
GATHERS_T = 4


def width(c):
    return min(PER, FIELDS - PER * c)


def dve_steps(c):
    return sum(width(k) for k in range(c + 1) if k not in ACT_CHUNKS)


def act_steps(c):
    return sum(1 for k in range(c + 1) if k in ACT_CHUNKS)


def sel_slot(k):
    return 4 + 4 * k


def mm_slot(k):
    return 9 + 4 * k


class Count:

    def __init__(self, engine, block):
        self.engine, self.block, self.bases = engine, block, {}

    def at(self, per_block, value):
        if isinstance(self.block, int):
            return per_block * self.block + value
        if per_block not in self.bases:
            self.bases[per_block] = self.engine.snap(self.block * per_block)
        return self.bases[per_block] + value

    def wait(self, sem, per_block, value):
        v = self.at(per_block, value)
        if not isinstance(v, int) or v > 0:
            self.engine.wait_ge(sem, v)


def cin_kernel(nc, ids, tables, dense_t, sel, mask, ident, ident_b, w0ab, b0, w1, b1, w2, b2,
               wt1, bt1, wt2, bt2, wt3, out):
    fp32, f32r, bf16 = mybir.dt.float32, mybir.dt.float32r, mybir.dt.bfloat16
    ALU, ACT = mybir.AluOpType, mybir.ActivationFunctionType

    ctx = ExitStack()
    with ctx:
        def sb(name, shape, dt=fp32):
            return ctx.enter_context(nc.sbuf_tensor(name, shape, dt))

        def pb(name, shape, dt=fp32):
            return ctx.enter_context(nc.psum_tensor(name, shape, dt))

        def sem(name):
            return ctx.enter_context(nc.semaphore(name))

        sel_sb = sb("sel_sb", [ROWS, PAIR_K + 1, ROWS], bf16)
        mask_sb = sb("mask_sb", [PART, BATCH_T])
        ident_sb = sb("ident_sb", [PART, PART])
        identb_sb = sb("identb_sb", [PART, PART], bf16)
        w0_sb = sb("w0_sb", [ROWS, PAIR_K, MAPS])
        w1_hi = sb("w1_hi", [PART, FIELDS * MAPS], f32r)
        w1_lo = sb("w1_lo", [PART, FIELDS * MAPS], f32r)
        w2_sb = sb("w2_sb", [PART, FIELDS, MAPS])
        b0_col = sb("b0_col", [PART, 1])
        b1_row = sb("b1_row", [PART, MAPS])
        b2_col = sb("b2_col", [PART, 1])
        b2_16 = sb("b2_16", [PART, 1])
        wt1_sb = sb("wt1_sb", [PART, 2, HIDDEN1])
        wt1_ctx = sb("wt1_ctx", [DIM, HIDDEN1])
        wt2_sb = sb("wt2_sb", [PART, HIDDEN1 // PART, HIDDEN2])
        wt3_sb = sb("wt3_sb", [PART, HIDDEN2 // PART])
        bt1_col = sb("bt1_col", [PART, HIDDEN1 // PART])
        bt2_col = sb("bt2_col", [PART, HIDDEN2 // PART])
        dense_sb = sb("dense_sb", [DIM, BATCH])
        idx = sb("idx", [PART, FIELDS], mybir.dt.int32)
        emb = sb("emb", [PART, FIELDS * DIM])
        emb_rest = sb("emb_rest", [PART, FIELDS * DIM])
        emb3 = sb("emb3", [PART, ROWS, DIM], bf16)
        x0_parts = sb("x0_parts", [ROWS, BATCH * DIM], bf16)
        x0_rep = sb("x0_rep", [ROWS, GROUP_N])
        x0_t = sb("x0_t", [PART, 2, TILES_G, COLS])
        pair = sb("pair", [ROWS, 2, GROUP_N])
        x1_hi = [sb(f"x1_hi{g}", [PART, GROUP_N], f32r) for g in range(2)]
        x1_lo = [sb(f"x1_lo{g}", [PART, GROUP_N], f32r) for g in range(2)]
        act_part = sb("act_part", [PART, 2, ACT_FIELDS, MAPS])
        dve_part = sb("dve_part", [PART, 2, 2, MAPS])
        x2_t = sb("x2_t", [PART, TILES_G, MAPS])
        x0_diag = sb("x0_diag", [PART, TILES_G, COLS, BATCH_T])
        p_sb = sb("p_sb", [PART, COLS, PART])
        z = sb("z", [PART, 2, BATCH])
        y_sb = sb("y_sb", [1, BATCH])
        w1_raw = p_sb[:, :, :].rearrange("p a b -> p (a b)")
        w0_raw = act_part[0:ROWS, :, :, :].rearrange("p a b c -> p (a b c)")[:, 0:2 * PAIR_K * MAPS] \
            .rearrange("p (a k) -> p a k", a=2)
        hid1 = p_sb[:, 0:4 * HIDDEN1 // PART, :].rearrange("p a b -> p (a b)").rearrange("p (m n) -> p m n", m=4)
        hid2 = p_sb[:, 16:24, :].rearrange("p a b -> p (a b)").rearrange("p (m n) -> p m n", m=2)

        t_ps = pb("t_ps", [PART, BANKS, 512])
        sel_ps = pb("sel_ps", [PART, 512])
        x1_ps = pb("x1_ps", [PART, 512])
        p_ps = pb("p_ps", [PART, 512])
        sh_ps = pb("sh_ps", [PART, 512])
        sh_b = sh_ps[:, :].bitcast(bf16)

        s_const = sem("s_const")
        s_w1 = sem("s_w1")
        s_late = sem("s_late")
        s_idx = sem("s_idx")
        s_emb = sem("s_emb")
        s_set = sem("s_set")
        s_whi = sem("s_whi")
        s_wlo = sem("s_wlo")
        s_b2 = sem("s_b2")
        s_part = sem("s_part")
        s_rest = sem("s_rest")
        s_sel = sem("s_sel")
        s_rep = sem("s_rep")
        s_pair = sem("s_pair")
        s_mm0 = sem("s_mm0")
        s_xhi = sem("s_xhi")
        s_xlo = sem("s_xlo")
        s_x0t = sem("s_x0t")
        s_sh = sem("s_sh")
        s_shfree = sem("s_shfree")
        s_t = sem("s_t")
        s_acc = sem("s_acc")
        s_act = sem("s_act")
        s_sum = sem("s_sum")
        s_x2 = sem("s_x2")
        s_diag = sem("s_diag")
        s_p = sem("s_p")
        s_pe = sem("s_pe")
        s_z1 = sem("s_z1")
        s_top = sem("s_top")
        s_hid = sem("s_hid")
        s_out = sem("s_out")

        def shared_use(n, j):
            if isinstance(n.block, int) and n.block == 0 and j == 0:
                return 0, 3
            return 7, 2 + j

        G4 = GROUPS_B
        T16 = TILES_B
        block = ctx.enter_context(nc.Block())

        @block.sync
        def _(sp):
            sp.dma_start(idx[:, :], ids[0:PART, :]).then_inc(s_idx, 16)
            consts = [(sel_sb[:, :, :], sel), (mask_sb[:, :], mask), (ident_sb[:, :], ident),
                      (identb_sb[:, :], ident_b), (w0_raw, w0ab),
                      (b0_col[:, :], b0.rearrange("(p a) -> p a", a=1)),
                      (b2_col[:, :], b2.rearrange("(p a) -> p a", a=1)),
                      (b1_row[:, :], b1.rearrange("(a s) -> a s", a=1).broadcast_to([PART, MAPS]))]
            for dst, src in consts:
                sp.dma_start(dst, src).then_inc(s_const, 16)
            w1_v = w1.rearrange("(i j) s -> j i s", j=PART)
            sp.dma_start(w1_raw[:, 0:FIELDS * MAPS].rearrange("p (i s) -> p i s", s=MAPS), w1_v).then_inc(s_w1, 16)
            late = [(w2_sb[:, :, :], w2.rearrange("(i j) s -> j i s", j=PART)),
                    (wt1_sb[:, :, :], wt1[0:2 * PART, :].rearrange("(k p) m -> p k m", p=PART)),
                    (wt1_ctx[:, :], wt1[2 * PART:2 * PART + DIM, :]),
                    (wt2_sb[:, :, :], wt2.rearrange("(k p) m -> p k m", p=PART)),
                    (wt3_sb[:, :], wt3),
                    (bt1_col[:, :], bt1),
                    (bt2_col[:, :], bt2),
                    (dense_sb[:, :], dense_t)]
            for dst, src in late:
                sp.dma_start(dst, src).then_inc(s_late, 16)

            def next_indices(b):
                n = Count(sp, b)
                n.wait(s_emb, 16 * FIELDS, 16 * FIELDS)
                row = (b + 1) * PART if isinstance(b, int) else sp.snap((b + 1) * PART)
                sp.dma_start(idx[:, :], ids[bass.ds(row, PART), :]).then_inc(s_idx, 16)

            next_indices(0)
            with sp.Fori(1, BLOCKS - 1) as b:
                next_indices(b)
            sp.wait_ge(s_hid, 2 * (6 + 1))
            sp.dma_start(out.rearrange("n a -> a n"), y_sb[:, :]).then_inc(s_out, 16)
            sp.wait_ge(s_out, 16)

        @block.gpsimd
        def _(pool):
            def gather(f):
                pool.indirect_dma_start(emb[:, f * DIM:(f + 1) * DIM], None, tables[f],
                                        bass.IndirectOffsetOnAxis(ap=idx[:, f:f + 1], axis=0)).then_inc(s_emb, 16)

            def diagonal(n, tile):
                g, t = divmod(tile, TILES_G)
                n.wait(s_x0t, G4, g + 1)
                n.wait(s_p, T16, tile - TILES_G + 1)
                pool.tensor_tensor(x0_diag[:, t, :, :],
                                   x0_t[:, g % 2, t, :].unsqueeze(2).broadcast_to([PART, COLS, BATCH_T]),
                                   mask_sb[:, :].unsqueeze(1).broadcast_to([PART, COLS, BATCH_T]),
                                   ALU.mult).then_inc(s_diag, 1)

            def sum_parts(n, tile):
                u, v = act_part[:, tile % 2, :, :], dve_part[:, tile % 2, :, :]
                n.wait(s_act, 3 * T16, 3 * tile + 2)
                pool.tensor_tensor(u[:, 0:4, :], u[:, 0:4, :], u[:, 4:8, :], ALU.add).then_inc(s_sum, 1)
                n.wait(s_act, 3 * T16, 3 * tile + 3)
                n.wait(s_sum, 4 * T16, 4 * tile + 1)
                pool.tensor_tensor(u[:, 0:4, :], u[:, 0:4, :], u[:, 8:12, :], ALU.add).then_inc(s_sum, 1)
                n.wait(s_sum, 4 * T16, 4 * tile + 2)
                pool.tensor_tensor(u[:, 0:2, :], u[:, 0:2, :], u[:, 2:4, :], ALU.add).then_inc(s_sum, 1)
                n.wait(s_acc, DVE_FIELDS * T16, DVE_FIELDS * (tile + 1))
                n.wait(s_sum, 4 * T16, 4 * tile + 3)
                pool.tensor_tensor(u[:, 0:2, :], u[:, 0:2, :], v, ALU.add).then_inc(s_sum, 1)
                n.wait(s_sum, 4 * T16, 4 * tile + 4)
                n.wait(s_p, T16, tile - TILES_G + 1)
                pool.tensor_tensor(x2_t[:, tile % TILES_G, :], u[:, 0, :], u[:, 1, :], ALU.add).then_inc(s_x2, 1)

            def body(b, last=False):
                n = Count(pool, b)
                for tile in range(TILES_B):
                    if not last and tile == 0:
                        n.wait(s_idx, 16, 32)
                        n.wait(s_rest, 2, 2)
                    diagonal(n, tile)
                    if not last:
                        for f in range(GATHERS_T * tile, min(GATHERS_T * (tile + 1), FIELDS)):
                            gather(f)
                    sum_parts(n, tile)

            pool.wait_ge(s_idx, 16)
            for f in range(FIELDS):
                gather(f)
            pool.wait_ge(s_const, 16 * 8)
            body(0)
            with pool.Fori(1, BLOCKS - 1) as b:
                body(b)
            body(BLOCKS - 1, last=True)

        @block.scalar
        def _(act):
            def parts(n):
                e3 = emb3[:, :, :].rearrange("p a d -> p (a d)")
                w = FIELDS * DIM
                n.wait(s_emb, 16 * FIELDS, 2 * 16 * FIELDS)
                n.wait(s_sh, 7, 2 if isinstance(n.block, int) and n.block == 0 else 1)
                act.activation(e3[:, 0:w], emb[:, :], ACT.Copy).then_inc(s_part, 1)
                n.wait(s_rest, 2, 3)
                act.activation(e3[:, w:2 * w], emb_rest[:, :], ACT.Copy).then_inc(s_part, 1)

            act.wait_ge(s_w1, 16)
            for c in range(CHUNKS):
                a, e = c * PER * MAPS, min((c + 1) * PER, FIELDS) * MAPS
                act.activation(w1_hi[:, a:e], w1_raw[:, a:e], ACT.Copy).then_inc(s_whi, 1)
            act.wait_ge(s_const, 16 * 8)
            act.activation(b2_16[:, :], b2_col[:, :], ACT.Copy, scale=float(DIM)).then_inc(s_b2, 1)

            def x0_parts_out(n, nxt, half, use):
                n.wait(s_sh, *use)
                start = (n.block + nxt) * BLOCK_N
                if not isinstance(start, int):
                    start = act.snap(start)
                dst = x0_parts[:, bass.ds(start, BLOCK_N)].rearrange("p (b d) -> p d b", d=DIM)
                src = sh_b[0:ROWS, :].rearrange("p (d b) -> p d b", b=PART)
                act.activation(dst[:, 8 * half:8 * half + 8, :], src, ACT.Copy).then_inc(s_shfree, 1)

            def rep_out(n, g):
                n.wait(s_sel, 8 * G4, 8 * g + 1)
                n.wait(s_pair, 7 * G4, 7 * g)
                n.wait(s_x0t, G4, g)
                act.activation(x0_rep[:, :], sel_ps[0:ROWS, :], ACT.Copy).then_inc(s_rep, 1)

            def x0t_out(n, g, use):
                n.wait(s_sh, *use)
                n.wait(s_acc, DVE_FIELDS * T16, DVE_FIELDS * TILES_G * (g - 1))
                n.wait(s_act, 3 * T16, 3 * TILES_G * (g - 1))
                n.wait(s_diag, T16, TILES_G * (g - 1))
                src = sh_ps[:, :].rearrange("p (t r) -> p t r", t=TILES_G)[:, :, 0:FIELDS]
                act.activation(x0_t[:, g % 2, :, 0:FIELDS], src, ACT.Copy).then_inc(s_x0t, 1)

            def x1_high(n, g):
                n.wait(s_mm0, 7 * G4, 7 * (g + 1))
                n.wait(s_t, CHUNKS * T16, CHUNKS * TILES_G * (g - 1))
                act.activation(x1_hi[g % 2][:, :], x1_ps[:, :], ACT.Identity, bias=b0_col[:, :]).then_inc(s_xhi, 1)

            def scale_chunk(n, tile, c):
                g, t = divmod(tile, TILES_G)
                n.wait(s_t, CHUNKS * T16, CHUNKS * tile + c + 1)
                if c == ACT_CHUNKS[0]:
                    n.wait(s_x0t, G4, g + 1)
                    n.wait(s_x2, T16, tile - 1)
                for w in range(PER):
                    i = PER * c + w
                    ins = act.activation(act_part[:, tile % 2, PER * ACT_CHUNKS.index(c) + w, :],
                                         t_ps[:, (CHUNKS * tile + c) % BANKS, w * MAPS:(w + 1) * MAPS],
                                         ACT.Copy, scale=x0_t[:, g % 2, t, i:i + 1])
                ins.then_inc(s_act, 1)

            def p_out(n, tile, first_block):
                n.wait(s_p, T16, tile + 1)
                if tile == 0 and not first_block:
                    n.wait(s_sh, *shared_use(n, 1)[:1], shared_use(n, 1)[1] + 1)
                    n.wait(s_z1, 1, 0)
                b = BATCH_T * (tile % TILES_B)
                act.activation(p_sb[:, :, b:b + BATCH_T],
                               p_ps[:, 0:COLS * BATCH_T].rearrange("p (i b) -> p i b", b=BATCH_T),
                               ACT.Copy).then_inc(s_pe, 1)

            def z_out(n, which, done, use=None):
                start = (n.block - 1) * PART
                if not isinstance(start, int):
                    start = act.snap(start)
                if which == 0:
                    n.wait(s_pe, *done)
                    act.activation(z[:, 0, bass.ds(start, PART)], p_sb[:, FIELDS, :], ACT.Copy).then_inc(s_z1, 1)
                else:
                    n.wait(s_sh, *use)
                    act.activation(z[:, 1, bass.ds(start, PART)], sh_ps[:, 0:PART], ACT.Identity,
                                   bias=b2_16[:, :]).then_inc(s_shfree, 1)

            def filled(n, j):
                per, value = shared_use(n, j)
                return per, value + 1

            def body(b, last=False):
                n = Count(act, b)
                first = isinstance(b, int) and b == 0
                for slot in range(TILES_B * CHUNKS):
                    tile, c = divmod(slot, CHUNKS)
                    g, sg = divmod(slot, SLOTS_G)
                    ahead = not (last and g == GROUPS_B - 1)
                    if c in ACT_CHUNKS:
                        scale_chunk(n, tile, c)
                    if sg == 0 and ahead:
                        rep_out(n, g + 1)
                    if sg == 5 and ahead:
                        x0t_out(n, g + 1, filled(n, (0, 2, 3, 6)[g]))
                    if sg == mm_slot(PAIR_K - 1) + 1 and ahead:
                        x1_high(n, g + 1)
                    if c == 4 and not (first and tile < LAG):
                        p_out(n, tile - LAG, first)
                    if not first and slot == Z_FIRST:
                        z_out(n, 0, (T16, 0))
                    if not first and slot == Z_FIRST + Z_SLOTS - 1:
                        z_out(n, 1, None, filled(n, 1))
                    if not last and slot == PREP_SLOTS[0] - 8:
                        parts(n)
                    if not last and slot in PREP_SLOTS:
                        half = PREP_SLOTS.index(slot)
                        x0_parts_out(n, 1, half, filled(n, 4 + half))

            start = Count(act, 0)
            act.wait_ge(s_emb, 16 * FIELDS)
            e3 = emb3[:, :, :].rearrange("p a d -> p (a d)")
            act.activation(e3[:, 0:FIELDS * DIM], emb[:, :], ACT.Copy).then_inc(s_part, 1)
            act.wait_ge(s_rest, 1)
            act.activation(e3[:, FIELDS * DIM:2 * FIELDS * DIM], emb_rest[:, :], ACT.Copy).then_inc(s_part, 1)
            for half in range(2):
                x0_parts_out(start, 0, half, (0, half + 1))
            rep_out(start, 0)
            x0t_out(start, 0, (0, 3))
            x1_high(start, 0)
            body(0)
            with act.Fori(1, BLOCKS - 1) as b:
                body(b)
            body(BLOCKS - 1, last=True)
            end = Count(act, BLOCKS)
            for tile in (-2, -1):
                p_out(end, tile, True)
            z_out(end, 0, (T16, 0))
            act.wait_ge(s_sh, 7 * (BLOCKS - 1) + 2 + 4 + 1)
            act.activation(z[:, 1, BATCH - PART:BATCH], sh_ps[:, 0:PART], ACT.Identity,
                           bias=b2_16[:, :]).then_inc(s_shfree, 1)
            act.wait_ge(s_late, 16 * 8)
            for half in range(2):
                base = 7 * half
                for m in range(4):
                    act.wait_ge(s_top, base + m + 1)
                    if m == 0 and half == 1:
                        act.wait_ge(s_top, 6)
                    act.activation(hid1[:, m, :], t_ps[:, m, :], ACT.Relu, bias=bt1_col[:, m:m + 1]).then_inc(s_hid, 1)
                for m in range(2):
                    act.wait_ge(s_top, base + 4 + m + 1)
                    if m == 0 and half == 1:
                        act.wait_ge(s_top, 7)
                    act.activation(hid2[:, m, :], (sel_ps, x1_ps)[m][:, :], ACT.Relu,
                                   bias=bt2_col[:, m:m + 1]).then_inc(s_hid, 1)
                act.wait_ge(s_top, base + 7)
                act.activation(y_sb[:, 512 * half:512 * half + 512], p_ps[0:1, :], ACT.Copy).then_inc(s_hid, 1)

        @block.tensor
        def _(pe):
            def chunk(n, tile, c):
                g, t = divmod(tile, TILES_G)
                seq = CHUNKS * tile + c
                if c == 0 and t == 0:
                    n.wait(s_xhi, G4, g + 1)
                    n.wait(s_xlo, G4, g + 1)
                back_tile, back_c = divmod(seq - BANKS, CHUNKS)
                if back_c in ACT_CHUNKS:
                    n.wait(s_act, 3 * T16, 3 * back_tile + act_steps(back_c))
                else:
                    n.wait(s_acc, DVE_FIELDS * T16, DVE_FIELDS * back_tile + dve_steps(back_c))
                cols = slice(c * PER * MAPS, (c * PER + width(c)) * MAPS)
                dst = t_ps[:, seq % BANKS, 0:width(c) * MAPS]
                hi, lo = (x[g % 2][:, t * PART:(t + 1) * PART] for x in (x1_hi, x1_lo))
                pe.matmul(dst, hi, w1_hi[:, cols], start=True, stop=False)
                pe.matmul(dst, hi, w1_lo[:, cols], start=False, stop=False)
                pe.matmul(dst, lo, w1_hi[:, cols], start=False, stop=True).then_inc(s_t, 1)

            def select(n, g, k):
                if k == 1:
                    n.wait(s_rep, G4, g + 1)
                else:
                    n.wait(s_pair, 7 * G4, 7 * g + (k - 1 if k else 0))
                if g == GROUPS_B:
                    n.wait(s_shfree, 3, 4)
                start = n.block * BLOCK_N + g * GROUP_N
                if not isinstance(start, int):
                    start = pe.snap(start)
                pe.matmul(sel_ps[0:ROWS, :], sel_sb[:, k, :], x0_parts[:, bass.ds(start, GROUP_N)],
                          start=True, stop=True).then_inc(s_sel, 1)

            def layer0(n, g, k):
                n.wait(s_pair, 7 * G4, 7 * g + k + 1)
                if k == 0:
                    n.wait(s_xlo, G4, g)
                pe.matmul(x1_ps[:, :], w0_sb[:, k, :], pair[:, (7 * g + k) % 2, :], start=(k == 0),
                          stop=(k == PAIR_K - 1)).then_inc(s_mm0, 1)

            def turn_x0(n, g, use, before_x0t):
                n.wait(s_rep, G4, g + 1)
                for t in range(TILES_G):
                    ins = pe.transpose(sh_ps[:, t * PART:t * PART + ROWS], x0_rep[:, t * PART:(t + 1) * PART],
                                       ident_sb[0:ROWS, 0:ROWS])
                ins.then_inc(s_sh, 1)

            def turn_parts(half):
                for d in range(8):
                    ins = pe.transpose(sh_b[0:ROWS, d * PART:(d + 1) * PART], emb3[:, :, 8 * half + d],
                                       identb_sb[:, :])
                ins.then_inc(s_sh, 1)

            def products(n, tile):
                n.wait(s_x2, T16, tile + 1)
                n.wait(s_diag, T16, tile + 1)
                n.wait(s_pe, T16, tile)
                t = tile % TILES_G
                pe.matmul(p_ps[:, 0:COLS * BATCH_T], x2_t[:, t, :],
                          x0_diag[:, t, :, :].rearrange("p i b -> p (i b)"), start=True, stop=True).then_inc(s_p, 1)

            def layer2(fields):
                for i in fields:
                    ins = pe.matmul(sh_ps[:, 0:PART], w2_sb[:, i, :], p_sb[:, i, :], start=(i == 0),
                                    stop=(i == FIELDS - 1))
                if i == FIELDS - 1:
                    ins.then_inc(s_sh, 1)

            def bank_free(n, x0t, other):
                n.wait(s_x0t, G4, x0t)
                n.wait(s_shfree, 3, other)

            def body(b, last=False):
                n = Count(pe, b)
                first = isinstance(b, int) and b == 0
                for slot in range(TILES_B * CHUNKS):
                    tile, c = divmod(slot, CHUNKS)
                    g, sg = divmod(slot, SLOTS_G)
                    ahead = not (last and g == GROUPS_B - 1)
                    chunk(n, tile, c)
                    if ahead:
                        if sg == 0:
                            select(n, g + 1, 0)
                        if sg == 4:
                            bank_free(n, g + 1, (1, 2, 2, 4)[g])
                            turn_x0(n, g + 1, None, None)
                        for k in range(PAIR_K):
                            if sg == mm_slot(k):
                                layer0(n, g + 1, k)
                            if sg == sel_slot(k):
                                select(n, g + 1, k + 1)
                    if c == 2 and not (first and tile < LAG):
                        products(n, tile - LAG)
                    if not first and Z_FIRST <= slot < Z_FIRST + Z_SLOTS:
                        if slot == Z_FIRST:
                            n.wait(s_pe, T16, 0)
                            bank_free(n, 2, 1)
                        k = Z_PER * (slot - Z_FIRST)
                        layer2(range(k, min(k + Z_PER, FIELDS)))
                    if not last and slot in PREP_SLOTS:
                        half = PREP_SLOTS.index(slot)
                        n.wait(s_part, 2, 4)
                        n.wait(s_rest, 2, 4)
                        bank_free(n, 4, 2 + half)
                        turn_parts(half)

            start = Count(pe, 0)
            pe.wait_ge(s_const, 16 * 8)
            pe.wait_ge(s_part, 2)
            pe.wait_ge(s_rest, 2)
            for half in range(2):
                if half:
                    pe.wait_ge(s_shfree, 1)
                turn_parts(half)
            pe.wait_ge(s_shfree, 2)
            select(start, 0, 0)
            turn_x0(start, 0, None, None)
            pe.wait_ge(s_set, 2)
            for k in range(PAIR_K):
                select(start, 0, k + 1)
                layer0(start, 0, k)
            pe.wait_ge(s_wlo, CHUNKS)
            body(0)
            pe.wait_ge(s_late, 16 * 8)
            with pe.Fori(1, BLOCKS - 1) as b:
                body(b)
            body(BLOCKS - 1, last=True)
            end = Count(pe, BLOCKS)
            for tile in (-2, -1):
                products(end, tile)
            end.wait(s_pe, T16, 0)
            pe.wait_ge(s_shfree, 3 * (BLOCKS - 1) + 2)
            pe.wait_ge(s_x0t, G4 * BLOCKS)
            layer2(range(FIELDS))
            pe.wait_ge(s_z1, BLOCKS)
            pe.wait_ge(s_shfree, 3 * (BLOCKS - 1) + 3)
            pe.wait_ge(s_acc, DVE_FIELDS * T16 * BLOCKS)
            pe.wait_ge(s_act, 3 * T16 * BLOCKS)
            pe.wait_ge(s_pe, T16 * BLOCKS)
            for half in range(2):
                cols = slice(512 * half, 512 * half + 512)
                for m in range(4):
                    mc = slice(m * PART, (m + 1) * PART)
                    if half:
                        pe.wait_ge(s_hid, m + 1)
                    pe.matmul(t_ps[:, m, :], wt1_sb[:, 0, mc], z[:, 0, cols], start=True, stop=False)
                    pe.matmul(t_ps[:, m, :], wt1_sb[:, 1, mc], z[:, 1, cols], start=False, stop=False)
                    pe.matmul(t_ps[:, m, :], wt1_ctx[:, mc], dense_sb[:, cols], start=False, stop=True).then_inc(s_top, 1)
                for m in range(2):
                    mc = slice(m * PART, (m + 1) * PART)
                    for k in range(4):
                        pe.wait_ge(s_hid, 7 * half + k + 1)
                        ins = pe.matmul((sel_ps, x1_ps)[m][:, :], wt2_sb[:, k, mc], hid1[:, k, :],
                                        start=(k == 0), stop=(k == 3))
                    ins.then_inc(s_top, 1)
                for k in range(2):
                    pe.wait_ge(s_hid, 7 * half + 4 + k + 1)
                    ins = pe.matmul(p_ps[0:1, :], wt3_sb[:, k:k + 1], hid2[:, k, :], start=(k == 0), stop=(k == 1))
                ins.then_inc(s_top, 1)

        @block.vector
        def _(dve):
            def pair_product(n, g, k):
                n.wait(s_sel, 8 * G4, 8 * g + k + 2)
                n.wait(s_rep, G4, g + 1)
                n.wait(s_mm0, 7 * G4, 7 * g + k - 1)
                dve.tensor_tensor(pair[:, (7 * g + k) % 2, :], sel_ps[0:ROWS, :], x0_rep[:, :], ALU.mult).then_inc(s_pair, 1)

            def x1_low(n, g):
                n.wait(s_xhi, G4, g + 1)
                n.wait(s_t, CHUNKS * T16, CHUNKS * TILES_G * (g - 1))
                dve.scalar_tensor_tensor(out=x1_lo[g % 2][:, :], in0=x1_ps[:, :], scalar=b0_col[:, :],
                                         in1=x1_hi[g % 2][:, :].bitcast(fp32), op0=ALU.add,
                                         op1=ALU.subtract).then_inc(s_xlo, 1)

            def rest(n, nxt):
                e3 = emb3[:, :, :].rearrange("p a d -> p (a d)")
                w = FIELDS * DIM
                n.wait(s_part, 2, 2 * nxt + 1)
                dve.tensor_tensor(emb_rest[:, :], emb[:, :], e3[:, 0:w], ALU.subtract).then_inc(s_rest, 1)
                n.wait(s_part, 2, 2 * nxt + 2)
                n.wait(s_rest, 2, 2 * nxt + 1)
                dve.tensor_tensor(e3[:, 2 * w:3 * w], emb_rest[:, :], e3[:, w:2 * w], ALU.subtract).then_inc(s_rest, 1)

            def add_chunk(n, tile, c):
                g, t = divmod(tile, TILES_G)
                n.wait(s_t, CHUNKS * T16, CHUNKS * tile + c + 1)
                if c == 0:
                    n.wait(s_x0t, G4, g + 1)
                    n.wait(s_sum, 4 * T16, 4 * (tile - 1))
                for w in range(width(c)):
                    step = dve_steps(c) - width(c) + w
                    acc = dve_part[:, tile % 2, step % 2, :]
                    src = t_ps[:, (CHUNKS * tile + c) % BANKS, w * MAPS:(w + 1) * MAPS]
                    x0 = x0_t[:, g % 2, t, PER * c + w:PER * c + w + 1]
                    if step == 0:
                        ins = dve.scalar_tensor_tensor(out=acc, in0=src, scalar=x0, in1=b1_row[:, :],
                                                       op0=ALU.mult, op1=ALU.add)
                    elif step == 1:
                        ins = dve.tensor_scalar(acc, src, x0, None, ALU.mult)
                    else:
                        n.wait(s_acc, DVE_FIELDS * T16, DVE_FIELDS * tile + step - 1)
                        ins = dve.scalar_tensor_tensor(out=acc, in0=src, scalar=x0, in1=acc,
                                                       op0=ALU.mult, op1=ALU.add)
                    ins.then_inc(s_acc, 1)

            def body(b, last=False):
                n = Count(dve, b)
                for slot in range(TILES_B * CHUNKS):
                    tile, c = divmod(slot, CHUNKS)
                    g, sg = divmod(slot, SLOTS_G)
                    ahead = not (last and g == GROUPS_B - 1)
                    if c not in ACT_CHUNKS:
                        add_chunk(n, tile, c)
                    if ahead:
                        for k in range(PAIR_K):
                            if sg == sel_slot(k):
                                pair_product(n, g + 1, k)
                        if sg == mm_slot(PAIR_K - 1) + 2:
                            x1_low(n, g + 1)
                    if not last and slot == PREP_SLOTS[0] - 8:
                        rest(n, 1)

            dve.memset(x0_t[:, :, :, FIELDS:COLS], 1.0).then_inc(s_set, 1)
            dve.wait_ge(s_const, 16 * 8)
            dve.tensor_tensor(w0_sb[:, :, :].rearrange("p k s -> p (k s)"), w0_raw[:, 0, :], w0_raw[:, 1, :],
                              ALU.add).then_inc(s_set, 1)
            for c in range(CHUNKS):
                a, e = c * PER * MAPS, min((c + 1) * PER, FIELDS) * MAPS
                dve.wait_ge(s_whi, c + 1)
                dve.tensor_tensor(w1_lo[:, a:e], w1_raw[:, a:e], w1_hi[:, a:e].bitcast(fp32),
                                  ALU.subtract).then_inc(s_wlo, 1)
            start = Count(dve, 0)
            rest(start, 0)
            for k in range(PAIR_K):
                pair_product(start, 0, k)
            x1_low(start, 0)
            body(0)
            with dve.Fori(1, BLOCKS - 1) as b:
                body(b)
            body(BLOCKS - 1, last=True)


def kernel(**inputs):
    import numpy as np
    import ml_dtypes
    import concourse.bacc as bacc
    from concourse.bass_utils import run_bass_kernel_spmd

    nc = bacc.Bacc("TRN2", target_bir_lowering=False, num_devices=1)
    arrays = {}

    def dram(name, a):
        a = np.ascontiguousarray(a)
        arrays[name] = a
        return nc.dram_tensor(name, a.shape, mybir.dt.from_np(a.dtype), kind="ExternalInput").ap()

    field = np.arange(FIELDS)
    sel = np.zeros((3, FIELDS, PAIR_K + 1, SHIFTS, FIELDS), ml_dtypes.bfloat16)
    for r in range(SHIFTS):
        sel[:, field, 0, r, field] = 1
    first, second = [], []
    for delta in range(DELTAS):
        k, r = divmod(delta, SHIFTS)
        sel[:, (field + delta) % FIELDS, 1 + k, r, field] = 1
        first.append(field)
        second.append((field + delta) % FIELDS)
    mask = np.repeat(np.eye(BATCH_T, dtype=np.float32), DIM, axis=0)
    w0 = np.asarray(inputs["L0_rec_w0"]).reshape(FIELDS, FIELDS, MAPS)
    i, j = np.stack(first), np.stack(second)
    w0ab = np.zeros((2, PAIR_K * SHIFTS, FIELDS, MAPS), np.float32)
    w0ab[0, :DELTAS] = w0[i, j]
    w0ab[1, 1:DELTAS] = w0[j[1:], i[1:]]
    w0ab = w0ab.reshape(2, PAIR_K, ROWS, MAPS).transpose(2, 0, 1, 3).reshape(ROWS, 2, PAIR_K * MAPS)

    args = [dram("ids", np.asarray(inputs["ids"])),
            [dram(f"tbl_{f}", np.asarray(inputs[f"tbl_{f}"])) for f in range(FIELDS)],
            dram("dense_t", np.asarray(inputs["dense_ctx"]).T),
            dram("sel", sel.reshape(ROWS, PAIR_K + 1, ROWS)), dram("mask", mask),
            dram("ident", np.eye(PART, dtype=np.float32)),
            dram("ident_b", np.eye(PART).astype(ml_dtypes.bfloat16)), dram("w0ab", w0ab)]
    for name in ("L0_rec_b0", "L0_rec_w1", "L0_rec_b1", "L0_rec_w2", "L0_rec_b2", "W_top1", "b_top1", "W_top2",
                 "b_top2", "W_top3"):
        a = np.asarray(inputs[name])
        if name in ("b_top1", "b_top2", "W_top3"):
            a = a.reshape(-1, PART).T
        args.append(dram(name, a))
    out = nc.dram_tensor("out_0", (BATCH, 1), mybir.dt.float32, kind="ExternalOutput").ap()
    cin_kernel(nc, *args, out)
    r = run_bass_kernel_spmd(nc, [arrays], core_ids=[0])
    return r.results[0]["out_0"]
```

```python
from contextlib import ExitStack

import concourse.bass as bass
from concourse import mybir

FIELDS, DIM, BATCH, MAPS = 39, 16, 1024, 128
PART = 128
TILES_G = 4
GROUPS_B = 4
TILES_B = TILES_G * GROUPS_B
BLOCKS = BATCH // PART
BATCH_T = PART // DIM
GROUP_N = TILES_G * PART
BLOCK_N = PART * DIM
DELTAS = FIELDS // 2 + 1
SHIFTS = 3
ROWS = SHIFTS * FIELDS
PAIR_K = -(-DELTAS // SHIFTS)
PER = 4
CHUNKS = -(-FIELDS // PER)
BANKS = 4
ACT_CHUNKS = (0, 3, 5, 8)
ACT_C = len(ACT_CHUNKS)
SUMS = 5
ACT_FIELDS = PER * len(ACT_CHUNKS)
DVE_FIELDS = FIELDS - ACT_FIELDS
COLS = FIELDS + 1
LAG = 2
SLOTS_G = TILES_G * CHUNKS
HIDDEN1, HIDDEN2 = 512, 256
Z_FIRST, Z_SLOTS, Z_PER = 17, 8, 5
PART_SLOTS = (94, 96, 98, 100)
PREP_SLOTS = (103, 109)
REP_SLOT = 37
GATHERS_T = 3
EARLY_TILE = 11
EARLY = GATHERS_T * (TILES_B - EARLY_TILE)
TOP_SLOT = 121
TOP_PIECES = ((0, 256), (256, 512), (512, 768), (768, 896), (896, 1024))
TOP_STEPS = HIDDEN1 // PART + HIDDEN2 // PART + 1


def width(c):
    return min(PER, FIELDS - PER * c)


def dve_steps(c):
    return sum(width(k) for k in range(c + 1) if k not in ACT_CHUNKS)


def act_steps(c):
    return sum(1 for k in range(c + 1) if k in ACT_CHUNKS)


def sel_slot(k):
    return 2 + 4 * k


def high_slot(k):
    return 4 + 4 * k


def low_slot(k):
    return 5 + 4 * k


def mm_slot(k):
    return 9 + 4 * k


def top_steps(slot):
    span, steps = TILES_B * CHUNKS - 1 - TOP_SLOT, (len(TOP_PIECES) - 1) * TOP_STEPS

    def before(at):
        return min(steps, max(0, at - TOP_SLOT) * steps // span)

    return range(before(slot), before(slot + 1))


class Count:

    def __init__(self, engine, block):
        self.engine, self.block, self.bases = engine, block, {}

    def at(self, per_block, value):
        if isinstance(self.block, int):
            return per_block * self.block + value
        if per_block not in self.bases:
            self.bases[per_block] = self.engine.snap(self.block * per_block)
        return self.bases[per_block] + value

    def wait(self, sem, per_block, value):
        v = self.at(per_block, value)
        if not isinstance(v, int) or v > 0:
            self.engine.wait_ge(sem, v)


def cin_kernel(nc, ids, tables, dense_t, sel, mask, ident, ident_b, w0ab, b0, w1, b1, w2, b2,
               wt1, bt1, wt2, bt2, wt3, out):
    fp32, f32r, bf16 = mybir.dt.float32, mybir.dt.float32r, mybir.dt.bfloat16
    ALU, ACT = mybir.AluOpType, mybir.ActivationFunctionType

    ctx = ExitStack()
    with ctx:
        def sb(name, shape, dt=fp32):
            return ctx.enter_context(nc.sbuf_tensor(name, shape, dt))

        def pb(name, shape, dt=fp32):
            return ctx.enter_context(nc.psum_tensor(name, shape, dt))

        def sem(name):
            return ctx.enter_context(nc.semaphore(name))

        sel_sb = sb("sel_sb", [ROWS, PAIR_K + 1, ROWS], bf16)
        mask_sb = sb("mask_sb", [PART, BATCH_T])
        ident_sb = sb("ident_sb", [PART, PART])
        identb_sb = sb("identb_sb", [PART, PART], bf16)
        w0_hi = sb("w0_hi", [ROWS, PAIR_K * MAPS], f32r)
        w0_lo = sb("w0_lo", [ROWS, PAIR_K * MAPS], f32r)
        w1_hi = sb("w1_hi", [PART, FIELDS * MAPS], f32r)
        w1_lo = sb("w1_lo", [PART, FIELDS * MAPS], f32r)
        w2_sb = sb("w2_sb", [PART, FIELDS, MAPS])
        b0_col = sb("b0_col", [PART, 1])
        b1_row = sb("b1_row", [PART, MAPS])
        b2_col = sb("b2_col", [PART, 1])
        b2_16 = sb("b2_16", [PART, 1])
        wt1_sb = sb("wt1_sb", [PART, 2, HIDDEN1])
        wt1_ctx = sb("wt1_ctx", [DIM, HIDDEN1])
        wt2_sb = sb("wt2_sb", [PART, HIDDEN1 // PART, HIDDEN2])
        wt3_sb = sb("wt3_sb", [PART, HIDDEN2 // PART])
        bt1_col = sb("bt1_col", [PART, HIDDEN1 // PART])
        bt2_col = sb("bt2_col", [PART, HIDDEN2 // PART])
        dense_sb = sb("dense_sb", [DIM, BATCH])
        idx = sb("idx", [PART, FIELDS], mybir.dt.int32)
        emb = sb("emb", [PART, FIELDS * DIM])
        emb_rest = sb("emb_rest", [PART, FIELDS * DIM])
        emb3 = sb("emb3", [PART, ROWS, DIM], bf16)
        x0_parts = sb("x0_parts", [ROWS, BATCH * DIM], bf16)
        x0_rep = sb("x0_rep", [ROWS, GROUP_N])
        x0_t = sb("x0_t", [PART, 2, TILES_G, COLS])
        pair = sb("pair", [ROWS, 2, GROUP_N])
        pair_hi = sb("pair_hi", [ROWS, 2, GROUP_N], f32r)
        pair_lo = sb("pair_lo", [ROWS, 2, GROUP_N], f32r)
        x1_hi = [sb(f"x1_hi{g}", [PART, GROUP_N], f32r) for g in range(2)]
        x1_lo = [sb(f"x1_lo{g}", [PART, GROUP_N], f32r) for g in range(2)]
        act_part = sb("act_part", [PART, 2, ACT_FIELDS, MAPS])
        dve_part = sb("dve_part", [PART, 2, 2, MAPS])
        x2_t = sb("x2_t", [PART, TILES_G, MAPS])
        x0_diag = sb("x0_diag", [PART, TILES_G, COLS, BATCH_T])
        p_sb = sb("p_sb", [PART, COLS, PART])
        z = sb("z", [PART, 2, BATCH])
        y_sb = sb("y_sb", [1, BATCH])
        hid1 = sb("hid1", [PART, HIDDEN1 // PART, 256])
        w1_raw = p_sb[:, :, :].rearrange("p a b -> p (a b)")
        w0_raw = act_part[0:ROWS, :, :, :].rearrange("p a b c -> p (a b c)")[:, 0:2 * PAIR_K * MAPS] \
            .rearrange("p (a k) -> p a k", a=2)
        hid2 = emb[:, 0:512].rearrange("p (m n) -> p m n", m=2)
        w0_sum = pair[:, :, :].rearrange("p a n -> p (a n)")[:, 0:PAIR_K * MAPS]

        t_ps = pb("t_ps", [PART, BANKS, 512])
        sel_ps = pb("sel_ps", [PART, 512])
        x1_ps = pb("x1_ps", [PART, 512])
        p_ps = pb("p_ps", [PART, 512])
        sh_ps = pb("sh_ps", [PART, 512])
        sh_b = sh_ps[:, :].bitcast(bf16)

        s_const = sem("s_const")
        s_w1 = sem("s_w1")
        s_late = sem("s_late")
        s_idx = sem("s_idx")
        s_emb = sem("s_emb")
        s_set = sem("s_set")
        s_whi = sem("s_whi")
        s_wlo = sem("s_wlo")
        s_w0hi = sem("s_w0hi")
        s_w0lo = sem("s_w0lo")
        s_b2 = sem("s_b2")
        s_part = sem("s_part")
        s_rest = sem("s_rest")
        s_sel = sem("s_sel")
        s_rep = sem("s_rep")
        s_pair = sem("s_pair")
        s_phi = sem("s_phi")
        s_plo = sem("s_plo")
        s_mm0 = sem("s_mm0")
        s_xhi = sem("s_xhi")
        s_xlo = sem("s_xlo")
        s_x0t = sem("s_x0t")
        s_sh = sem("s_sh")
        s_shfree = sem("s_shfree")
        s_t = sem("s_t")
        s_acc = sem("s_acc")
        s_join = sem("s_join")
        s_act = sem("s_act")
        s_sum = sem("s_sum")
        s_x2 = sem("s_x2")
        s_diag = sem("s_diag")
        s_p = sem("s_p")
        s_pe = sem("s_pe")
        s_z1 = sem("s_z1")
        s_top = sem("s_top")
        s_hid = sem("s_hid")
        s_out = sem("s_out")

        def shared_use(n, j):
            if isinstance(n.block, int) and n.block == 0 and j == 0:
                return 0, 3
            return 7, 2 + j

        G4 = GROUPS_B
        T16 = TILES_B
        block = ctx.enter_context(nc.Block())

        @block.sync
        def _(sp):
            sp.dma_start(idx[:, :], ids[0:PART, :]).then_inc(s_idx, 16)
            consts = [(sel_sb[:, :, :], sel), (mask_sb[:, :], mask), (ident_sb[:, :], ident),
                      (identb_sb[:, :], ident_b), (w0_raw, w0ab),
                      (b0_col[:, :], b0.rearrange("(p a) -> p a", a=1)),
                      (b2_col[:, :], b2.rearrange("(p a) -> p a", a=1)),
                      (b1_row[:, :], b1.rearrange("(a s) -> a s", a=1).broadcast_to([PART, MAPS]))]
            for dst, src in consts:
                sp.dma_start(dst, src).then_inc(s_const, 16)
            w1_v = w1.rearrange("(i j) s -> j i s", j=PART)
            sp.dma_start(w1_raw[:, 0:FIELDS * MAPS].rearrange("p (i s) -> p i s", s=MAPS), w1_v).then_inc(s_w1, 16)
            late = [(w2_sb[:, :, :], w2.rearrange("(i j) s -> j i s", j=PART)),
                    (wt1_sb[:, :, :], wt1[0:2 * PART, :].rearrange("(k p) m -> p k m", p=PART)),
                    (wt1_ctx[:, :], wt1[2 * PART:2 * PART + DIM, :]),
                    (wt2_sb[:, :, :], wt2.rearrange("(k p) m -> p k m", p=PART)),
                    (wt3_sb[:, :], wt3),
                    (bt1_col[:, :], bt1),
                    (bt2_col[:, :], bt2),
                    (dense_sb[:, :], dense_t)]
            for dst, src in late:
                sp.dma_start(dst, src).then_inc(s_late, 16)

            def next_indices(b):
                n = Count(sp, b)
                n.wait(s_emb, 16 * FIELDS, 16 * FIELDS)
                row = (b + 1) * PART if isinstance(b, int) else sp.snap((b + 1) * PART)
                sp.dma_start(idx[:, :], ids[bass.ds(row, PART), :]).then_inc(s_idx, 16)

            next_indices(0)
            with sp.Fori(1, BLOCKS - 1) as b:
                next_indices(b)
            sp.wait_ge(s_hid, TOP_STEPS * len(TOP_PIECES))
            sp.dma_start(out.rearrange("n a -> a n"), y_sb[:, :]).then_inc(s_out, 16)
            sp.wait_ge(s_out, 16)

        @block.gpsimd
        def _(pool):
            def gather(f):
                pool.indirect_dma_start(emb[:, f * DIM:(f + 1) * DIM], None, tables[f],
                                        bass.IndirectOffsetOnAxis(ap=idx[:, f:f + 1], axis=0)).then_inc(s_emb, 16)

            def diagonal(n, tile):
                g, t = divmod(tile, TILES_G)
                n.wait(s_x0t, G4, g + 1)
                n.wait(s_p, T16, tile - TILES_G + 1)
                pool.tensor_tensor(x0_diag[:, t, :, :],
                                   x0_t[:, g % 2, t, :].unsqueeze(2).broadcast_to([PART, COLS, BATCH_T]),
                                   mask_sb[:, :].unsqueeze(1).broadcast_to([PART, COLS, BATCH_T]),
                                   ALU.mult).then_inc(s_diag, 1)

            def sum_parts(n, tile):
                u = act_part[:, tile % 2, :, :]

                def add(step, to, of, count):
                    if step:
                        n.wait(s_sum, SUMS * T16, SUMS * tile + step)
                    pool.tensor_tensor(u[:, to:to + count, :], u[:, to:to + count, :], u[:, of:of + count, :],
                                       ALU.add).then_inc(s_sum, 1)

                n.wait(s_act, ACT_C * T16, ACT_C * tile + 3)
                add(0, 4, 8, 4)
                n.wait(s_act, ACT_C * T16, ACT_C * tile + 4)
                add(1, 4, 12, 4)
                add(2, 4, 6, 2)
                add(3, 2, 4, 2)
                n.wait(s_join, T16, tile + 1)
                add(4, 0, 2, 2)
                n.wait(s_sum, SUMS * T16, SUMS * (tile + 1))
                n.wait(s_p, T16, tile - TILES_G + 1)
                pool.tensor_tensor(x2_t[:, tile % TILES_G, :], u[:, 0, :], u[:, 1, :], ALU.add).then_inc(s_x2, 1)

            def body(b, rest=True, early=True):
                n = Count(pool, b)
                for tile in range(TILES_B):
                    starts = early and tile == EARLY_TILE
                    if starts:
                        n.wait(s_idx, 16, 48)
                        n.wait(s_rest, 2, 4)
                    diagonal(n, tile)
                    if rest and tile < EARLY_TILE:
                        for f in range(EARLY + GATHERS_T * tile, min(EARLY + GATHERS_T * (tile + 1), FIELDS)):
                            gather(f)
                    if early and tile >= EARLY_TILE:
                        for f in range(GATHERS_T * (tile - EARLY_TILE), GATHERS_T * (tile - EARLY_TILE + 1)):
                            gather(f)
                    sum_parts(n, tile)

            pool.wait_ge(s_idx, 16)
            for f in range(FIELDS):
                gather(f)
            pool.wait_ge(s_idx, 32)
            pool.wait_ge(s_rest, 2)
            for f in range(EARLY):
                gather(f)
            pool.wait_ge(s_const, 16 * 8)
            body(0)
            with pool.Fori(1, BLOCKS - 2) as b:
                body(b)
            body(BLOCKS - 2, early=False)
            body(BLOCKS - 1, rest=False, early=False)

        @block.scalar
        def _(act):
            def part_high(n):
                n.wait(s_emb, 16 * FIELDS, 2 * 16 * FIELDS)
                n.wait(s_sh, 7, 2 if isinstance(n.block, int) and n.block == 0 else 1)
                act.activation(e3[:, 0:w], emb[:, :], ACT.Copy).then_inc(s_part, 1)

            def part_middle(n):
                n.wait(s_rest, 2, 3)
                act.activation(e3[:, w:2 * w], emb_rest[:, :], ACT.Copy).then_inc(s_part, 1)

            e3, w = emb3[:, :, :].rearrange("p a d -> p (a d)"), FIELDS * DIM
            act.wait_ge(s_set, 2)
            act.activation(w0_hi[:, :], w0_sum, ACT.Copy).then_inc(s_w0hi, 1)
            act.wait_ge(s_w1, 16)
            for c in range(CHUNKS):
                a, e = c * PER * MAPS, min((c + 1) * PER, FIELDS) * MAPS
                act.activation(w1_hi[:, a:e], w1_raw[:, a:e], ACT.Copy).then_inc(s_whi, 1)
            act.wait_ge(s_const, 16 * 8)
            act.activation(b2_16[:, :], b2_col[:, :], ACT.Copy, scale=float(DIM)).then_inc(s_b2, 1)

            def x0_parts_out(n, nxt, half, use):
                n.wait(s_sh, *use)
                start = (n.block + nxt) * BLOCK_N
                if not isinstance(start, int):
                    start = act.snap(start)
                dst = x0_parts[:, bass.ds(start, BLOCK_N)].rearrange("p (b d) -> p d b", d=DIM)
                src = sh_b[0:ROWS, :].rearrange("p (d b) -> p d b", b=PART)
                act.activation(dst[:, 8 * half:8 * half + 8, :], src, ACT.Copy).then_inc(s_shfree, 1)

            def rep_out(n, g):
                n.wait(s_sel, 8 * G4, 8 * g + 1)
                n.wait(s_pair, 7 * G4, 7 * g)
                n.wait(s_x0t, G4, g)
                act.activation(x0_rep[:, :], sel_ps[0:ROWS, :], ACT.Copy).then_inc(s_rep, 1)

            def x0t_out(n, g, use):
                n.wait(s_sh, *use)
                n.wait(s_acc, DVE_FIELDS * T16, DVE_FIELDS * TILES_G * (g - 1))
                n.wait(s_act, ACT_C * T16, ACT_C * TILES_G * (g - 1))
                n.wait(s_diag, T16, TILES_G * (g - 1))
                src = sh_ps[:, :].rearrange("p (t r) -> p t r", t=TILES_G)[:, :, 0:FIELDS]
                act.activation(x0_t[:, g % 2, :, 0:FIELDS], src, ACT.Copy).then_inc(s_x0t, 1)

            def pair_high(n, g, k):
                n.wait(s_pair, 7 * G4, 7 * g + k + 1)
                n.wait(s_mm0, 7 * G4, 7 * g + k - 1)
                half = (7 * g + k) % 2
                act.activation(pair_hi[:, half, :], pair[:, half, :], ACT.Copy).then_inc(s_phi, 1)

            def x1_high(n, g):
                n.wait(s_mm0, 7 * G4, 7 * (g + 1))
                n.wait(s_t, CHUNKS * T16, CHUNKS * TILES_G * (g - 1))
                act.activation(x1_hi[g % 2][:, :], x1_ps[:, :], ACT.Identity, bias=b0_col[:, :]).then_inc(s_xhi, 1)

            def scale_chunk(n, tile, c):
                g, t = divmod(tile, TILES_G)
                n.wait(s_t, CHUNKS * T16, CHUNKS * tile + c + 1)
                if c == ACT_CHUNKS[0]:
                    n.wait(s_x0t, G4, g + 1)
                    n.wait(s_x2, T16, tile - 1)
                for w in range(PER):
                    i = PER * c + w
                    ins = act.activation(act_part[:, tile % 2, PER * ACT_CHUNKS.index(c) + w, :],
                                         t_ps[:, (CHUNKS * tile + c) % BANKS, w * MAPS:(w + 1) * MAPS],
                                         ACT.Copy, scale=x0_t[:, g % 2, t, i:i + 1])
                ins.then_inc(s_act, 1)

            def p_out(n, tile, first_block):
                n.wait(s_p, T16, tile + 1)
                if tile == 0 and not first_block:
                    n.wait(s_sh, *shared_use(n, 1)[:1], shared_use(n, 1)[1] + 1)
                    n.wait(s_z1, 1, 0)
                b = BATCH_T * (tile % TILES_B)
                act.activation(p_sb[:, :, b:b + BATCH_T],
                               p_ps[:, 0:COLS * BATCH_T].rearrange("p (i b) -> p i b", b=BATCH_T),
                               ACT.Copy).then_inc(s_pe, 1)

            def z_out(n, which, done, use=None):
                start = (n.block - 1) * PART
                if not isinstance(start, int):
                    start = act.snap(start)
                if which == 0:
                    n.wait(s_pe, *done)
                    act.activation(z[:, 0, bass.ds(start, PART)], p_sb[:, FIELDS, :], ACT.Copy).then_inc(s_z1, 1)
                else:
                    n.wait(s_sh, *use)
                    act.activation(z[:, 1, bass.ds(start, PART)], sh_ps[:, 0:PART], ACT.Identity,
                                   bias=b2_16[:, :]).then_inc(s_shfree, 1)

            def top_out(step):
                piece, m = divmod(step, TOP_STEPS)
                a, e = TOP_PIECES[piece]
                src = (sel_ps, x1_ps)[step % 2]
                act.wait_ge(s_top, step + 1)
                if m < 4:
                    ins = act.activation(hid1[:, m, 0:e - a], src[:, 0:e - a], ACT.Relu, bias=bt1_col[:, m:m + 1])
                elif m < 6:
                    ins = act.activation(hid2[:, m - 4, 0:e - a], src[:, 0:e - a], ACT.Relu,
                                         bias=bt2_col[:, m - 4:m - 3])
                else:
                    ins = act.activation(y_sb[:, a:e], src[0:1, 0:e - a], ACT.Copy)
                ins.then_inc(s_hid, 1)

            def filled(n, j):
                per, value = shared_use(n, j)
                return per, value + 1

            def body(b, last=False):
                n = Count(act, b)
                first = isinstance(b, int) and b == 0
                for slot in range(TILES_B * CHUNKS):
                    tile, c = divmod(slot, CHUNKS)
                    g, sg = divmod(slot, SLOTS_G)
                    ahead = not (last and g == GROUPS_B - 1)
                    if c in ACT_CHUNKS:
                        scale_chunk(n, tile, c)
                    if sg == REP_SLOT + 1 and not (last and g >= GROUPS_B - 2):
                        rep_out(n, g + 2)
                    if sg == 5 and ahead:
                        x0t_out(n, g + 1, filled(n, (0, 2, 3, 6)[g]))
                    for k in range(PAIR_K):
                        if sg == high_slot(k) and ahead:
                            pair_high(n, g + 1, k)
                    if sg == mm_slot(PAIR_K - 1) + 1 and ahead:
                        x1_high(n, g + 1)
                    if last:
                        for step in top_steps(slot - 1):
                            top_out(step)
                    if c == 4 and not (first and tile < LAG):
                        p_out(n, tile - LAG, first)
                    if not first and slot == Z_FIRST:
                        z_out(n, 0, (T16, 0))
                    if not first and slot == Z_FIRST + Z_SLOTS - 1:
                        z_out(n, 1, None, filled(n, 1))
                    if not last and slot == PART_SLOTS[0]:
                        part_high(n)
                    if not last and slot == PART_SLOTS[2]:
                        part_middle(n)
                    if not last and slot in PREP_SLOTS:
                        half = PREP_SLOTS.index(slot)
                        x0_parts_out(n, 1, half, filled(n, 4 + half))

            start = Count(act, 0)
            act.wait_ge(s_emb, 16 * FIELDS)
            act.activation(e3[:, 0:FIELDS * DIM], emb[:, :], ACT.Copy).then_inc(s_part, 1)
            act.wait_ge(s_rest, 1)
            act.activation(e3[:, FIELDS * DIM:2 * FIELDS * DIM], emb_rest[:, :], ACT.Copy).then_inc(s_part, 1)
            act.wait_ge(s_late, 16 * 8)
            for half in range(2):
                x0_parts_out(start, 0, half, (0, half + 1))
            rep_out(start, 0)
            x0t_out(start, 0, (0, 3))
            for k in range(PAIR_K):
                pair_high(start, 0, k)
            x1_high(start, 0)
            rep_out(start, 1)
            body(0)
            with act.Fori(1, BLOCKS - 1) as b:
                body(b)
            body(BLOCKS - 1, last=True)
            end = Count(act, BLOCKS)
            for tile in (-2, -1):
                p_out(end, tile, True)
            z_out(end, 0, (T16, 0))
            act.wait_ge(s_sh, 7 * (BLOCKS - 1) + 2 + 4 + 1)
            act.activation(z[:, 1, BATCH - PART:BATCH], sh_ps[:, 0:PART], ACT.Identity,
                           bias=b2_16[:, :]).then_inc(s_shfree, 1)
            for step in range((len(TOP_PIECES) - 1) * TOP_STEPS, len(TOP_PIECES) * TOP_STEPS):
                top_out(step)

        @block.tensor
        def _(pe):
            def chunk(n, tile, c):
                g, t = divmod(tile, TILES_G)
                seq = CHUNKS * tile + c
                if c == 0 and t == 0:
                    n.wait(s_xhi, G4, g + 1)
                    n.wait(s_xlo, G4, g + 1)
                back_tile, back_c = divmod(seq - BANKS, CHUNKS)
                if back_c in ACT_CHUNKS:
                    n.wait(s_act, ACT_C * T16, ACT_C * back_tile + act_steps(back_c))
                else:
                    n.wait(s_acc, DVE_FIELDS * T16, DVE_FIELDS * back_tile + dve_steps(back_c))
                cols = slice(c * PER * MAPS, (c * PER + width(c)) * MAPS)
                dst = t_ps[:, seq % BANKS, 0:width(c) * MAPS]
                hi, lo = (x[g % 2][:, t * PART:(t + 1) * PART] for x in (x1_hi, x1_lo))
                pe.matmul(dst, hi, w1_hi[:, cols], start=True, stop=False)
                pe.matmul(dst, hi, w1_lo[:, cols], start=False, stop=False)
                pe.matmul(dst, lo, w1_hi[:, cols], start=False, stop=True).then_inc(s_t, 1)

            def select(n, g, k):
                if k == 1:
                    n.wait(s_rep, G4, g + 1)
                else:
                    n.wait(s_pair, 7 * G4, 7 * g + (k - 1 if k else 0))
                if g == GROUPS_B and k == 0:
                    n.wait(s_shfree, 3, 4)
                start = n.block * BLOCK_N + g * GROUP_N
                if not isinstance(start, int):
                    start = pe.snap(start)
                pe.matmul(sel_ps[0:ROWS, :], sel_sb[:, k, :], x0_parts[:, bass.ds(start, GROUP_N)],
                          start=True, stop=True).then_inc(s_sel, 1)

            def layer0(n, g, k):
                n.wait(s_phi, 7 * G4, 7 * g + k + 1)
                n.wait(s_plo, 7 * G4, 7 * g + k + 1)
                if k == 0:
                    n.wait(s_xlo, G4, g)
                hi, lo = (x[:, k * MAPS:(k + 1) * MAPS] for x in (w0_hi, w0_lo))
                half = (7 * g + k) % 2
                pe.matmul(x1_ps[:, :], hi, pair_hi[:, half, :], start=(k == 0), stop=False)
                pe.matmul(x1_ps[:, :], hi, pair_lo[:, half, :], start=False, stop=False)
                pe.matmul(x1_ps[:, :], lo, pair_hi[:, half, :], start=False,
                          stop=(k == PAIR_K - 1)).then_inc(s_mm0, 1)

            def turn_x0(n, g):
                n.wait(s_rep, G4, g + 1)
                for t in range(TILES_G):
                    ins = pe.transpose(sh_ps[:, t * PART:t * PART + ROWS], x0_rep[:, t * PART:(t + 1) * PART],
                                       ident_sb[0:ROWS, 0:ROWS])
                ins.then_inc(s_sh, 1)

            def turn_parts(half):
                for d in range(8):
                    ins = pe.transpose(sh_b[0:ROWS, d * PART:(d + 1) * PART], emb3[:, :, 8 * half + d],
                                       identb_sb[:, :])
                ins.then_inc(s_sh, 1)

            def products(n, tile):
                n.wait(s_x2, T16, tile + 1)
                n.wait(s_diag, T16, tile + 1)
                n.wait(s_pe, T16, tile)
                t = tile % TILES_G
                pe.matmul(p_ps[:, 0:COLS * BATCH_T], x2_t[:, t, :],
                          x0_diag[:, t, :, :].rearrange("p i b -> p (i b)"), start=True, stop=True).then_inc(s_p, 1)

            def layer2(fields):
                for i in fields:
                    ins = pe.matmul(sh_ps[:, 0:PART], w2_sb[:, i, :], p_sb[:, i, :], start=(i == 0),
                                    stop=(i == FIELDS - 1))
                if i == FIELDS - 1:
                    ins.then_inc(s_sh, 1)

            def bank_free(n, x0t, other):
                n.wait(s_x0t, G4, x0t)
                n.wait(s_shfree, 3, other)

            def body(b, last=False):
                n = Count(pe, b)
                first = isinstance(b, int) and b == 0
                for slot in range(TILES_B * CHUNKS):
                    tile, c = divmod(slot, CHUNKS)
                    g, sg = divmod(slot, SLOTS_G)
                    ahead = not (last and g == GROUPS_B - 1)
                    chunk(n, tile, c)
                    if sg == REP_SLOT and not (last and g >= GROUPS_B - 2):
                        select(n, g + 2, 0)
                    if ahead:
                        if sg == 4:
                            bank_free(n, g + 1, (1, 2, 2, 4)[g])
                            turn_x0(n, g + 1)
                        for k in range(PAIR_K):
                            if sg == mm_slot(k):
                                layer0(n, g + 1, k)
                            if sg == sel_slot(k):
                                select(n, g + 1, k + 1)
                    if c == 2 and not (first and tile < LAG):
                        products(n, tile - LAG)
                    if not first and Z_FIRST <= slot < Z_FIRST + Z_SLOTS:
                        if slot == Z_FIRST:
                            n.wait(s_pe, T16, 0)
                            bank_free(n, 2, 1)
                        k = Z_PER * (slot - Z_FIRST)
                        layer2(range(k, min(k + Z_PER, FIELDS)))
                    if not last and slot in PREP_SLOTS:
                        half = PREP_SLOTS.index(slot)
                        n.wait(s_part, 2, 4)
                        n.wait(s_rest, 2, 4)
                        bank_free(n, 4, 2 + half)
                        turn_parts(half)
                    if last:
                        if slot == TOP_SLOT:
                            pe.wait_ge(s_pair, 7 * G4 * BLOCKS)
                            pe.wait_ge(s_xlo, G4 * BLOCKS)
                            pe.wait_ge(s_z1, BLOCKS - 1)
                            pe.wait_ge(s_shfree, 3 * (BLOCKS - 1) + 2)
                        for step in top_steps(slot):
                            top(step)

            def top(step):
                piece, m = divmod(step, TOP_STEPS)
                a, e = TOP_PIECES[piece]
                w = e - a
                dst = (sel_ps, x1_ps)[step % 2]
                if step >= 2:
                    pe.wait_ge(s_hid, step - 1)
                if m < 4:
                    mc = slice(m * PART, (m + 1) * PART)
                    pe.matmul(dst[:, 0:w], wt1_sb[:, 0, mc], z[:, 0, a:e], start=True, stop=False)
                    pe.matmul(dst[:, 0:w], wt1_sb[:, 1, mc], z[:, 1, a:e], start=False, stop=False)
                    ins = pe.matmul(dst[:, 0:w], wt1_ctx[:, mc], dense_sb[:, a:e], start=False, stop=True)
                elif m < 6:
                    mc = slice((m - 4) * PART, (m - 3) * PART)
                    pe.wait_ge(s_hid, TOP_STEPS * piece + 4)
                    for k in range(4):
                        ins = pe.matmul(dst[:, 0:w], wt2_sb[:, k, mc], hid1[:, k, 0:w], start=(k == 0), stop=(k == 3))
                else:
                    pe.wait_ge(s_hid, TOP_STEPS * piece + 6)
                    for k in range(2):
                        ins = pe.matmul(dst[0:1, 0:w], wt3_sb[:, k:k + 1], hid2[:, k, 0:w], start=(k == 0), stop=(k == 1))
                ins.then_inc(s_top, 1)

            start = Count(pe, 0)
            pe.wait_ge(s_const, 16 * 8)
            pe.wait_ge(s_part, 2)
            pe.wait_ge(s_rest, 2)
            for half in range(2):
                if half:
                    pe.wait_ge(s_shfree, 1)
                turn_parts(half)
            pe.wait_ge(s_shfree, 2)
            select(start, 0, 0)
            turn_x0(start, 0)
            pe.wait_ge(s_w0lo, 1)
            select(start, 0, 1)
            for k in range(PAIR_K):
                if k < PAIR_K - 1:
                    select(start, 0, k + 2)
                layer0(start, 0, k)
            select(start, 1, 0)
            pe.wait_ge(s_wlo, CHUNKS)
            body(0)
            pe.wait_ge(s_late, 16 * 8)
            with pe.Fori(1, BLOCKS - 1) as b:
                body(b)
            body(BLOCKS - 1, last=True)
            end = Count(pe, BLOCKS)
            for tile in (-2, -1):
                products(end, tile)
            end.wait(s_pe, T16, 0)
            pe.wait_ge(s_shfree, 3 * (BLOCKS - 1) + 2)
            pe.wait_ge(s_x0t, G4 * BLOCKS)
            layer2(range(FIELDS))
            pe.wait_ge(s_z1, BLOCKS)
            pe.wait_ge(s_shfree, 3 * (BLOCKS - 1) + 3)
            for step in range((len(TOP_PIECES) - 1) * TOP_STEPS, len(TOP_PIECES) * TOP_STEPS):
                top(step)

        @block.vector
        def _(dve):
            def pair_product(n, g, k):
                n.wait(s_sel, 8 * G4, 8 * g + k + 2)
                n.wait(s_rep, G4, g + 1)
                n.wait(s_phi, 7 * G4, 7 * g + k - 1)
                dve.tensor_tensor(pair[:, (7 * g + k) % 2, :], sel_ps[0:ROWS, :], x0_rep[:, :], ALU.mult).then_inc(s_pair, 1)

            def pair_low(n, g, k):
                n.wait(s_phi, 7 * G4, 7 * g + k + 1)
                n.wait(s_mm0, 7 * G4, 7 * g + k - 1)
                half = (7 * g + k) % 2
                dve.tensor_tensor(pair_lo[:, half, :], pair[:, half, :], pair_hi[:, half, :].bitcast(fp32),
                                  ALU.subtract).then_inc(s_plo, 1)

            def x1_low(n, g):
                n.wait(s_xhi, G4, g + 1)
                n.wait(s_t, CHUNKS * T16, CHUNKS * TILES_G * (g - 1))
                dve.scalar_tensor_tensor(out=x1_lo[g % 2][:, :], in0=x1_ps[:, :], scalar=b0_col[:, :],
                                         in1=x1_hi[g % 2][:, :].bitcast(fp32), op0=ALU.add,
                                         op1=ALU.subtract).then_inc(s_xlo, 1)

            def rest(n, nxt):
                n.wait(s_part, 2, 2 * nxt + 1)
                dve.tensor_tensor(emb_rest[:, :], emb[:, :], e3[:, 0:w], ALU.subtract).then_inc(s_rest, 1)

            def part_low(n, nxt):
                n.wait(s_part, 2, 2 * nxt + 2)
                n.wait(s_rest, 2, 2 * nxt + 1)
                dve.tensor_tensor(e3[:, 2 * w:3 * w], emb_rest[:, :], e3[:, w:2 * w], ALU.subtract).then_inc(s_rest, 1)

            def add_chunk(n, tile, c):
                g, t = divmod(tile, TILES_G)
                n.wait(s_t, CHUNKS * T16, CHUNKS * tile + c + 1)
                if dve_steps(c) == width(c):
                    n.wait(s_x0t, G4, g + 1)
                    n.wait(s_act, ACT_C * T16, ACT_C * tile + 1)
                for w in range(width(c)):
                    step = dve_steps(c) - width(c) + w
                    acc = dve_part[:, tile % 2, step % 2, :]
                    src = t_ps[:, (CHUNKS * tile + c) % BANKS, w * MAPS:(w + 1) * MAPS]
                    x0 = x0_t[:, g % 2, t, PER * c + w:PER * c + w + 1]
                    if step == 0:
                        ins = dve.scalar_tensor_tensor(out=acc, in0=src, scalar=x0, in1=b1_row[:, :],
                                                       op0=ALU.mult, op1=ALU.add)
                    elif step == 1:
                        ins = dve.scalar_tensor_tensor(out=acc, in0=src, scalar=x0, in1=act_part[:, tile % 2, 0, :],
                                                       op0=ALU.mult, op1=ALU.add)
                    else:
                        n.wait(s_acc, DVE_FIELDS * T16, DVE_FIELDS * tile + step - 1)
                        ins = dve.scalar_tensor_tensor(out=acc, in0=src, scalar=x0, in1=acc,
                                                       op0=ALU.mult, op1=ALU.add)
                    ins.then_inc(s_acc, 1)

            def join(n, tile):
                n.wait(s_acc, DVE_FIELDS * T16, DVE_FIELDS * (tile + 1))
                dve.tensor_tensor(act_part[:, tile % 2, 0, :], dve_part[:, tile % 2, 0, :],
                                  dve_part[:, tile % 2, 1, :], ALU.add).then_inc(s_join, 1)

            def body(b, last=False):
                n = Count(dve, b)
                first = isinstance(b, int) and b == 0
                for slot in range(TILES_B * CHUNKS):
                    tile, c = divmod(slot, CHUNKS)
                    g, sg = divmod(slot, SLOTS_G)
                    ahead = not (last and g == GROUPS_B - 1)
                    if c not in ACT_CHUNKS:
                        add_chunk(n, tile, c)
                    if c == 1 and not (first and tile == 0):
                        join(n, tile - 1)
                    if ahead:
                        for k in range(PAIR_K):
                            if sg == sel_slot(k):
                                pair_product(n, g + 1, k)
                            if sg == low_slot(k):
                                pair_low(n, g + 1, k)
                        if sg == mm_slot(PAIR_K - 1) + 2:
                            x1_low(n, g + 1)
                    if not last and slot == PART_SLOTS[1]:
                        rest(n, 1)
                    if not last and slot == PART_SLOTS[3]:
                        part_low(n, 1)

            e3, w = emb3[:, :, :].rearrange("p a d -> p (a d)"), FIELDS * DIM
            dve.memset(x0_t[:, :, :, FIELDS:COLS], 1.0).then_inc(s_set, 1)
            dve.wait_ge(s_const, 16 * 8)
            dve.tensor_tensor(w0_sum, w0_raw[:, 0, :], w0_raw[:, 1, :],
                              ALU.add).then_inc(s_set, 1)
            dve.wait_ge(s_w0hi, 1)
            dve.tensor_tensor(w0_lo[:, :], w0_sum, w0_hi[:, :].bitcast(fp32), ALU.subtract).then_inc(s_w0lo, 1)
            for c in range(CHUNKS):
                a, e = c * PER * MAPS, min((c + 1) * PER, FIELDS) * MAPS
                dve.wait_ge(s_whi, c + 1)
                dve.tensor_tensor(w1_lo[:, a:e], w1_raw[:, a:e], w1_hi[:, a:e].bitcast(fp32),
                                  ALU.subtract).then_inc(s_wlo, 1)
            start = Count(dve, 0)
            rest(start, 0)
            part_low(start, 0)
            pair_product(start, 0, 0)
            for k in range(PAIR_K):
                if k < PAIR_K - 1:
                    pair_product(start, 0, k + 1)
                pair_low(start, 0, k)
            x1_low(start, 0)
            body(0)
            with dve.Fori(1, BLOCKS - 1) as b:
                body(b)
            body(BLOCKS - 1, last=True)
            join(Count(dve, BLOCKS), -1)


def kernel(**inputs):
    import numpy as np
    import ml_dtypes
    import concourse.bacc as bacc
    from concourse.bass_utils import run_bass_kernel_spmd

    nc = bacc.Bacc("TRN2", target_bir_lowering=False, num_devices=1)
    arrays = {}

    def dram(name, a):
        a = np.ascontiguousarray(a)
        arrays[name] = a
        return nc.dram_tensor(name, a.shape, mybir.dt.from_np(a.dtype), kind="ExternalInput").ap()

    field = np.arange(FIELDS)
    sel = np.zeros((3, FIELDS, PAIR_K + 1, SHIFTS, FIELDS), ml_dtypes.bfloat16)
    for r in range(SHIFTS):
        sel[:, field, 0, r, field] = 1
    first, second = [], []
    for delta in range(DELTAS):
        k, r = divmod(delta, SHIFTS)
        sel[:, (field + delta) % FIELDS, 1 + k, r, field] = 1
        first.append(field)
        second.append((field + delta) % FIELDS)
    mask = np.repeat(np.eye(BATCH_T, dtype=np.float32), DIM, axis=0)
    w0 = np.asarray(inputs["L0_rec_w0"]).reshape(FIELDS, FIELDS, MAPS)
    i, j = np.stack(first), np.stack(second)
    w0ab = np.zeros((2, PAIR_K * SHIFTS, FIELDS, MAPS), np.float32)
    w0ab[0, :DELTAS] = w0[i, j]
    w0ab[1, 1:DELTAS] = w0[j[1:], i[1:]]
    w0ab = w0ab.reshape(2, PAIR_K, ROWS, MAPS).transpose(2, 0, 1, 3).reshape(ROWS, 2, PAIR_K * MAPS)

    args = [dram("ids", np.asarray(inputs["ids"])),
            [dram(f"tbl_{f}", np.asarray(inputs[f"tbl_{f}"])) for f in range(FIELDS)],
            dram("dense_t", np.asarray(inputs["dense_ctx"]).T),
            dram("sel", sel.reshape(ROWS, PAIR_K + 1, ROWS)), dram("mask", mask),
            dram("ident", np.eye(PART, dtype=np.float32)),
            dram("ident_b", np.eye(PART).astype(ml_dtypes.bfloat16)), dram("w0ab", w0ab)]
    for name in ("L0_rec_b0", "L0_rec_w1", "L0_rec_b1", "L0_rec_w2", "L0_rec_b2", "W_top1", "b_top1", "W_top2",
                 "b_top2", "W_top3"):
        a = np.asarray(inputs[name])
        if name in ("b_top1", "b_top2", "W_top3"):
            a = a.reshape(-1, PART).T
        args.append(dram(name, a))
    out = nc.dram_tensor("out_0", (BATCH, 1), mybir.dt.float32, kind="ExternalOutput").ap()
    cin_kernel(nc, *args, out)
    r = run_bass_kernel_spmd(nc, [arrays], core_ids=[0])
    return r.results[0]["out_0"]
```

```python
from contextlib import ExitStack

import concourse.bass as bass
from concourse import mybir

FIELDS, DIM, BATCH, MAPS = 39, 16, 1024, 128
PART = 128
TILES_G = 4
GROUPS_B = 4
TILES_B = TILES_G * GROUPS_B
BLOCKS = BATCH // PART
BATCH_T = PART // DIM
GROUP_N = TILES_G * PART
BLOCK_N = PART * DIM
DELTAS = FIELDS // 2 + 1
SHIFTS = 3
ROWS = SHIFTS * FIELDS
PAIR_K = -(-DELTAS // SHIFTS)
PER = 4
CHUNKS = -(-FIELDS // PER)
BANKS = 4
ACT_CHUNKS = (0, 2, 4, 6, 8)
ACT_C = len(ACT_CHUNKS)
SUMS = 5
ACT_FIELDS = sum(min(PER, FIELDS - PER * c) for c in ACT_CHUNKS)
DVE_FIELDS = FIELDS - ACT_FIELDS
COLS = FIELDS + 1
LAG = 2
SLOTS_G = TILES_G * CHUNKS
HIDDEN1, HIDDEN2 = 512, 256
Z_FIRST, Z_SLOTS, Z_PER = 17, 8, 5
WRAP = DELTAS + 1
HALVES = ((0, WRAP), (WRAP, FIELDS))
GATHER_TILE = 9
DIAG_SLOTS = (15, 17, 19, 21, 25, 27, 29, 31)
FOLD_C = 9
TOP_SLOT = 119
TOP_PIECES = ((0, 256), (256, 512), (512, 768), (768, 896), (896, 1024))
TOP_STEPS = HIDDEN1 // PART + HIDDEN2 // PART + 1
TOP_ALONE = (len(TOP_PIECES) - 1) * TOP_STEPS
TOP_EARLY = TOP_ALONE - 8


def width(c):
    return min(PER, FIELDS - PER * c)


def dve_steps(c):
    return sum(width(k) for k in range(c + 1) if k not in ACT_CHUNKS)


def act_steps(c):
    return sum(1 for k in range(c + 1) if k in ACT_CHUNKS)


def pair_slot(k):
    return 1 + 4 * k


def high_slot(k):
    return 3 + 4 * k


def low_slot(k):
    return 4 + 4 * k


def mm_slot(k):
    return 7 + 4 * k


def gathers(tile):
    j = (tile - GATHER_TILE) % TILES_B
    return range(FIELDS * j // TILES_B, FIELDS * (j + 1) // TILES_B)


def top_order():
    order = [(0, m) for m in range(4)]
    for p in range(1, len(TOP_PIECES) - 1):
        order += [(p, 0), (p, 1), (p - 1, 4), (p - 1, 5), (p, 2), (p, 3), (p - 1, 6)]
    order += [(len(TOP_PIECES) - 2, m) for m in (4, 5, 6)]
    return order + [(len(TOP_PIECES) - 1, m) for m in range(TOP_STEPS)]


TOP_ORDER = top_order()


def top_steps(slot):
    span, steps = TILES_B * CHUNKS - 1 - TOP_SLOT, TOP_EARLY

    def before(at):
        return min(steps, max(0, at - TOP_SLOT) * steps // span)

    return range(before(slot), before(slot + 1))


class Count:

    def __init__(self, engine, block):
        self.engine, self.block, self.bases = engine, block, {}

    def at(self, per_block, value):
        if isinstance(self.block, int):
            return per_block * self.block + value
        if per_block not in self.bases:
            self.bases[per_block] = self.engine.snap(self.block * per_block)
        return self.bases[per_block] + value

    def wait(self, sem, per_block, value):
        v = self.at(per_block, value)
        assert isinstance(v, int) or per_block + value > 0, "a loop starts at block 1"
        if not isinstance(v, int) or v > 0:
            self.engine.wait_ge(sem, v)


def cin_kernel(nc, ids, tables, dense_t, mask, ident, w0ab, b0, w1, b1, w2, b2,
               wt1, bt1, wt2, bt2, wt3, out):
    fp32, f32r = mybir.dt.float32, mybir.dt.float32r
    ALU, ACT = mybir.AluOpType, mybir.ActivationFunctionType

    ctx = ExitStack()
    with ctx:
        def sb(name, shape, dt=fp32):
            return ctx.enter_context(nc.sbuf_tensor(name, shape, dt))

        def pb(name, shape, dt=fp32):
            return ctx.enter_context(nc.psum_tensor(name, shape, dt))

        def sem(name):
            return ctx.enter_context(nc.semaphore(name))

        mask_sb = sb("mask_sb", [PART, BATCH_T])
        ident_sb = sb("ident_sb", [PART, PART])
        w0_hi = sb("w0_hi", [ROWS, PAIR_K * MAPS], f32r)
        w0_lo = sb("w0_lo", [ROWS, PAIR_K * MAPS], f32r)
        w1_hi = sb("w1_hi", [PART, FIELDS * MAPS], f32r)
        w1_lo = sb("w1_lo", [PART, FIELDS * MAPS], f32r)
        w2_sb = sb("w2_sb", [PART, FIELDS, MAPS])
        b0_col = sb("b0_col", [PART, 1])
        b1_row = sb("b1_row", [PART, MAPS])
        b2_col = sb("b2_col", [PART, 1])
        b2_16 = sb("b2_16", [PART, 1])
        wt1_sb = sb("wt1_sb", [PART, 2, HIDDEN1])
        wt1_ctx = sb("wt1_ctx", [DIM, HIDDEN1])
        wt2_sb = sb("wt2_sb", [PART, HIDDEN1 // PART, HIDDEN2])
        wt3_sb = sb("wt3_sb", [PART, HIDDEN2 // PART])
        bt1_col = sb("bt1_col", [PART, HIDDEN1 // PART])
        bt2_col = sb("bt2_col", [PART, HIDDEN2 // PART])
        dense_sb = sb("dense_sb", [DIM, BATCH])
        idx = sb("idx", [PART, FIELDS], mybir.dt.int32)
        emb = sb("emb", [PART, FIELDS * DIM])
        x0_dram = nc.dram_tensor("x0_dram", (FIELDS + WRAP, BATCH * DIM), fp32, kind="Internal").ap()
        x0_rep = [sb(f"x0_rep{g}", [ROWS, GROUP_N]) for g in range(2)]
        x0_shift = [sb(f"x0_shift{g}", [ROWS, PAIR_K, GROUP_N]) for g in range(2)]
        x0_t = sb("x0_t", [PART, 2, TILES_G, COLS])
        pair_hi = sb("pair_hi", [ROWS, 2, GROUP_N], f32r)
        pair_lo = sb("pair_lo", [ROWS, 2, GROUP_N], f32r)
        x1_hi = [sb(f"x1_hi{g}", [PART, GROUP_N], f32r) for g in range(2)]
        x1_lo = [sb(f"x1_lo{g}", [PART, GROUP_N], f32r) for g in range(2)]
        act_part = sb("act_part", [PART, 2, ACT_FIELDS, MAPS])
        dve_part = sb("dve_part", [PART, 2, 2, MAPS])
        x2_t = sb("x2_t", [PART, TILES_G, MAPS])
        x0_diag = sb("x0_diag", [PART, 2, TILES_G, COLS, BATCH_T])
        p_sb = sb("p_sb", [PART, COLS, PART])
        z = sb("z", [PART, 2, BATCH])
        y_sb = sb("y_sb", [1, BATCH])
        hid1 = sb("hid1", [PART, 2, HIDDEN1 // PART, 256])
        w1_raw = p_sb[:, :, :].rearrange("p a b -> p (a b)")
        w0_raw = act_part[0:ROWS, :, :, :].rearrange("p a b c -> p (a b c)")[:, 0:2 * PAIR_K * MAPS] \
            .rearrange("p (a k) -> p a k", a=2)
        hid2 = emb[:, 0:512].rearrange("p (m n) -> p m n", m=2)
        w0_sum = act_part[0:ROWS, :, :, :].rearrange("p a b c -> p (a b c)")[:, 2 * PAIR_K * MAPS:3 * PAIR_K * MAPS]

        t_ps = pb("t_ps", [PART, BANKS, 512])
        pair_ps = pb("pair_ps", [PART, 512])
        x1_ps = pb("x1_ps", [PART, 512])
        p_ps = pb("p_ps", [PART, 512])
        sh_ps = pb("sh_ps", [PART, 512])

        s_const = sem("s_const")
        s_w1 = sem("s_w1")
        s_late = sem("s_late")
        s_idx = [sem(f"s_idx{h}") for h in range(2)]
        s_emb = [sem(f"s_emb{h}") for h in range(2)]
        s_set = sem("s_set")
        s_whi = sem("s_whi")
        s_wlo = sem("s_wlo")
        s_w0hi = sem("s_w0hi")
        s_w0lo = sem("s_w0lo")
        s_b2 = sem("s_b2")
        s_store = sem("s_store")
        s_first = sem("s_first")
        s_second = sem("s_second")
        s_load = [sem(f"s_load{g}") for g in range(2)]
        s_pair = sem("s_pair")
        s_phi = sem("s_phi")
        s_plo = sem("s_plo")
        s_mm0 = sem("s_mm0")
        s_xhi = sem("s_xhi")
        s_xlo = sem("s_xlo")
        s_x0t = sem("s_x0t")
        s_sh = sem("s_sh")
        s_shfree = sem("s_shfree")
        s_t = sem("s_t")
        s_acc = sem("s_acc")
        s_fold = sem("s_fold")
        s_join = sem("s_join")
        s_act = sem("s_act")
        s_sum = sem("s_sum")
        s_x2 = sem("s_x2")
        s_diag = sem("s_diag")
        s_p = sem("s_p")
        s_pe = sem("s_pe")
        s_z1 = sem("s_z1")
        s_top = sem("s_top")
        s_hid = sem("s_hid")
        s_out = sem("s_out")

        def shared_use(n, j):
            if isinstance(n.block, int) and n.block == 0 and j == 0:
                return 0, 1
            return 5, j

        def pair_bank(n, g, k):
            if isinstance(n.block, int) and n.block == 0 and g == 0:
                return t_ps[0:ROWS, k % BANKS, :], BANKS
            return pair_ps[0:ROWS, :], 1

        G4 = GROUPS_B
        T16 = TILES_B
        block = ctx.enter_context(nc.Block())

        @block.sync
        def _(sp):
            for h, (lo, hi) in enumerate(HALVES):
                sp.dma_start(idx[:, lo:hi], ids[0:PART, lo:hi]).then_inc(s_idx[h], 16)
            consts = [(mask_sb[:, :], mask), (ident_sb[:, :], ident), (w0_raw, w0ab),
                      (b0_col[:, :], b0.rearrange("(p a) -> p a", a=1)),
                      (b2_col[:, :], b2.rearrange("(p a) -> p a", a=1)),
                      (b1_row[:, :], b1.rearrange("(a s) -> a s", a=1).broadcast_to([PART, MAPS]))]
            for dst, src in consts:
                sp.dma_start(dst, src).then_inc(s_const, 16)
            w1_v = w1.rearrange("(i j) s -> j i s", j=PART)
            sp.dma_start(w1_raw[:, 0:FIELDS * MAPS].rearrange("p (i s) -> p i s", s=MAPS), w1_v).then_inc(s_w1, 16)
            late = [(w2_sb[:, :, :], w2.rearrange("(i j) s -> j i s", j=PART)),
                    (wt1_sb[:, :, :], wt1[0:2 * PART, :].rearrange("(k p) m -> p k m", p=PART)),
                    (wt1_ctx[:, :], wt1[2 * PART:2 * PART + DIM, :]),
                    (wt2_sb[:, :, :], wt2.rearrange("(k p) m -> p k m", p=PART)),
                    (wt3_sb[:, :], wt3),
                    (bt1_col[:, :], bt1),
                    (bt2_col[:, :], bt2),
                    (dense_sb[:, :], dense_t)]
            for dst, src in late:
                sp.dma_start(dst, src).then_inc(s_late, 16)

            def at(value):
                return value if isinstance(value, int) else sp.snap(value)

            def next_indices(b, h):
                lo, hi = HALVES[h]
                start = at((b + 1) * (PART * FIELDS) + lo)
                sp.dma_start(idx[:, lo:hi],
                             bass.AP(ids.tensor, start, [[FIELDS, PART], [1, hi - lo]])).then_inc(s_idx[h], 16)

            def store(b, h):
                lo, hi = HALVES[h]
                cols, gathered = bass.ds(at(b * BLOCK_N), BLOCK_N), at((b + 1) * 16 * (hi - lo))
                sp.wait_ge(s_emb[h], gathered)
                for row in ((0, FIELDS), (WRAP,))[h]:
                    sp.dma_start(x0_dram[row:row + hi - lo, cols].rearrange("i (b d) -> b i d", d=DIM),
                                 emb[:, lo * DIM:hi * DIM].rearrange("b (i d) -> b i d", d=DIM)).then_inc(s_store, 16)
                if h == 0:
                    stored = at(b * 48 + 32)
                    sp.wait_ge(s_store, stored)

            def wait_free(b, g):
                pairs = at(b * 7 * G4 + 7 * (g - 1))
                sp.wait_ge(s_plo, pairs)

            def load_first():
                row = BATCH * DIM
                for (a, e), landed in (((0, 1), s_first), ((1, 3), s_second), ((3, 5), s_load[0]), ((5, PAIR_K), s_load[0])):
                    for r in range(SHIFTS):
                        rows = slice(r * FIELDS, (r + 1) * FIELDS)
                        if a == 0:
                            sp.dma_start(x0_rep[0][rows, :], x0_dram[0:FIELDS, 0:GROUP_N]).then_inc(s_first, 16)
                        src = bass.AP(x0_dram.tensor, (SHIFTS * a + r) * row,
                                      [[row, FIELDS], [SHIFTS * row, e - a], [1, GROUP_N]])
                        sp.dma_start(x0_shift[0][rows, a:e, :], src).then_inc(landed, 16)

            def load(b, g):
                row = BATCH * DIM
                starts = [at(b * BLOCK_N + (g * GROUP_N + r * row)) for r in range(SHIFTS)]
                for r in range(SHIFTS):
                    rows = slice(r * FIELDS, (r + 1) * FIELDS)
                    sp.dma_start(x0_rep[g % 2][rows, :],
                                 x0_dram[0:FIELDS, bass.ds(starts[0], GROUP_N)]).then_inc(s_load[g % 2], 16)
                    src = bass.AP(x0_dram.tensor, starts[r], [[row, FIELDS], [SHIFTS * row, PAIR_K], [1, GROUP_N]])
                    sp.dma_start(x0_shift[g % 2][rows, :, :], src).then_inc(s_load[g % 2], 16)

            def body(b, last=False):
                more = not (last or isinstance(b, int) and b == BLOCKS - 2)
                wait_free(b, 2)
                load(b, 2)
                if not last:
                    store(b + 1, 0)
                    if more:
                        next_indices(b + 1, 0)
                wait_free(b, 3)
                load(b, 3)
                if not last:
                    store(b + 1, 1)
                    wait_free(b, G4)
                    if more:
                        next_indices(b + 1, 1)
                    stored = at((b + 2) * 48)
                    sp.wait_ge(s_store, stored)
                    load(b, G4)
                    wait_free(b, G4 + 1)
                    load(b, G4 + 1)

            for h in range(2):
                store(0, h)
                next_indices(0, h)
            sp.wait_ge(s_store, 48)
            load_first()
            load(0, 1)
            body(0)
            with sp.Fori(1, BLOCKS - 2) as b:
                body(b)
            body(BLOCKS - 2)
            body(BLOCKS - 1, last=True)
            sp.wait_ge(s_hid, len(TOP_ORDER))
            sp.dma_start(out.rearrange("n a -> a n"), y_sb[:, :]).then_inc(s_out, 16)
            sp.wait_ge(s_out, 16)

        @block.gpsimd
        def _(pool):
            def gather(f):
                pool.indirect_dma_start(emb[:, f * DIM:(f + 1) * DIM], None, tables[f],
                                        bass.IndirectOffsetOnAxis(ap=idx[:, f:f + 1], axis=0)).then_inc(s_emb[f >= WRAP], 16)

            def sum_parts(n, tile):
                u = act_part[:, tile % 2, :, :]

                def add(step, to, of, count):
                    if step:
                        n.wait(s_sum, SUMS * T16, SUMS * tile + step)
                    pool.tensor_tensor(u[:, to:to + count, :], u[:, to:to + count, :], u[:, of:of + count, :],
                                       ALU.add).then_inc(s_sum, 1)

                n.wait(s_fold, T16, tile + 1)
                n.wait(s_act, ACT_C * T16, ACT_C * tile + 4)
                add(0, 4, 12, 4)
                n.wait(s_act, ACT_C * T16, ACT_C * tile + 5)
                add(1, 4, 16, 4)
                add(2, 4, 6, 2)
                add(3, 2, 4, 2)
                n.wait(s_join, T16, tile + 1)
                add(4, 0, 2, 2)
                n.wait(s_sum, SUMS * T16, SUMS * (tile + 1))
                n.wait(s_p, T16, tile - TILES_G + 1)
                pool.tensor_tensor(x2_t[:, tile % TILES_G, :], u[:, 0, :], u[:, 1, :], ALU.add).then_inc(s_x2, 1)

            def body(b, rest=True, early=True):
                n = Count(pool, b)
                for tile in range(TILES_B):
                    begins = tile >= GATHER_TILE
                    fields = gathers(tile) if (early if begins else rest) else range(0)
                    if 0 in fields:
                        n.wait(s_idx[0], 16, 48)
                        n.wait(s_store, 48, 80)
                    if WRAP in fields:
                        n.wait(s_idx[1], 16, 32)
                        n.wait(s_store, 48, 48)
                    sum_parts(n, tile)
                    for f in fields:
                        gather(f)

            for h, (lo, hi) in enumerate(HALVES):
                pool.wait_ge(s_idx[h], 16)
                for f in range(lo, hi):
                    gather(f)
            pool.wait_ge(s_idx[0], 32)
            pool.wait_ge(s_store, 32)
            for f in range(gathers(TILES_B - 1).stop):
                gather(f)
            pool.wait_ge(s_const, 16 * 6)
            body(0)
            with pool.Fori(1, BLOCKS - 2) as b:
                body(b)
            body(BLOCKS - 2, early=False)
            body(BLOCKS - 1, rest=False, early=False)

        @block.scalar
        def _(act):
            act.wait_ge(s_set, 2)
            act.activation(w0_hi[:, :], w0_sum, ACT.Copy).then_inc(s_w0hi, 1)
            act.wait_ge(s_w1, 16)
            for c in range(CHUNKS):
                a, e = c * PER * MAPS, min((c + 1) * PER, FIELDS) * MAPS
                act.activation(w1_hi[:, a:e], w1_raw[:, a:e], ACT.Copy).then_inc(s_whi, 1)
            act.wait_ge(s_const, 16 * 6)
            act.activation(b2_16[:, :], b2_col[:, :], ACT.Copy, scale=float(DIM)).then_inc(s_b2, 1)

            def x0t_out(n, g, use):
                n.wait(s_sh, *use)
                n.wait(s_acc, DVE_FIELDS * T16, DVE_FIELDS * TILES_G * (g - 1))
                n.wait(s_act, ACT_C * T16, ACT_C * TILES_G * (g - 1))
                n.wait(s_diag, BATCH_T * G4, BATCH_T * (g - 1))
                src = sh_ps[:, :].rearrange("p (t r) -> p t r", t=TILES_G)[:, :, 0:FIELDS]
                act.activation(x0_t[:, g % 2, :, 0:FIELDS], src, ACT.Copy).then_inc(s_x0t, 1)

            def diagonal(n, g, batch):
                if batch == 0:
                    n.wait(s_x0t, G4, g + 1)
                    n.wait(s_p, T16, TILES_G * (g - 1))
                act.activation(x0_diag[:, g % 2, :, :, batch], x0_t[:, g % 2, :, :], ACT.Copy,
                               scale=mask_sb[:, batch:batch + 1]).then_inc(s_diag, 1)

            def pair_high(n, g, k):
                n.wait(s_pair, 7 * G4, 7 * g + k + 1)
                n.wait(s_mm0, 7 * G4, 7 * g + k - 1)
                act.activation(pair_hi[:, (7 * g + k) % 2, :], pair_bank(n, g, k)[0], ACT.Copy).then_inc(s_phi, 1)

            def x1_high(n, g):
                n.wait(s_mm0, 7 * G4, 7 * (g + 1))
                n.wait(s_t, CHUNKS * T16, CHUNKS * TILES_G * (g - 1))
                act.activation(x1_hi[g % 2][:, :], x1_ps[:, :], ACT.Identity, bias=b0_col[:, :]).then_inc(s_xhi, 1)

            def scale_chunk(n, tile, c):
                g, t = divmod(tile, TILES_G)
                n.wait(s_t, CHUNKS * T16, CHUNKS * tile + c + 1)
                if c == ACT_CHUNKS[0]:
                    if t == 0:
                        n.wait(s_x0t, G4, g + 1)
                    n.wait(s_x2, T16, tile - 1)
                for w in range(width(c)):
                    i = PER * c + w
                    ins = act.activation(act_part[:, tile % 2, PER * ACT_CHUNKS.index(c) + w, :],
                                         t_ps[:, (CHUNKS * tile + c) % BANKS, w * MAPS:(w + 1) * MAPS],
                                         ACT.Copy, scale=x0_t[:, g % 2, t, i:i + 1])
                ins.then_inc(s_act, 1)

            def p_out(n, tile, first_block):
                n.wait(s_p, T16, tile + 1)
                if tile == 0 and not first_block:
                    n.wait(s_sh, *shared_use(n, 1)[:1], shared_use(n, 1)[1] + 1)
                    n.wait(s_z1, 1, 0)
                b = BATCH_T * (tile % TILES_B)
                act.activation(p_sb[:, :, b:b + BATCH_T],
                               p_ps[:, 0:COLS * BATCH_T].rearrange("p (i b) -> p i b", b=BATCH_T),
                               ACT.Copy).then_inc(s_pe, 1)

            def z_out(n, which, done, use=None):
                start = (n.block - 1) * PART
                if not isinstance(start, int):
                    start = act.snap(start)
                if which == 0:
                    n.wait(s_pe, *done)
                    act.activation(z[:, 0, bass.ds(start, PART)], p_sb[:, FIELDS, :], ACT.Copy).then_inc(s_z1, 1)
                else:
                    n.wait(s_sh, *use)
                    act.activation(z[:, 1, bass.ds(start, PART)], sh_ps[:, 0:PART], ACT.Identity,
                                   bias=b2_16[:, :]).then_inc(s_shfree, 1)

            def top_out(step):
                piece, m = TOP_ORDER[step]
                a, e = TOP_PIECES[piece]
                src = (pair_ps, x1_ps)[step % 2]
                act.wait_ge(s_top, step + 1)
                if m < 4:
                    ins = act.activation(hid1[:, piece % 2, m, 0:e - a], src[:, 0:e - a], ACT.Relu, bias=bt1_col[:, m:m + 1])
                elif m < 6:
                    ins = act.activation(hid2[:, m - 4, 0:e - a], src[:, 0:e - a], ACT.Relu,
                                         bias=bt2_col[:, m - 4:m - 3])
                else:
                    ins = act.activation(y_sb[:, a:e], src[0:1, 0:e - a], ACT.Copy)
                ins.then_inc(s_hid, 1)

            def filled(n, j):
                per, value = shared_use(n, j)
                return per, value + 1

            def body(b, last=False):
                n = Count(act, b)
                first = isinstance(b, int) and b == 0
                for slot in range(TILES_B * CHUNKS):
                    tile, c = divmod(slot, CHUNKS)
                    g, sg = divmod(slot, SLOTS_G)
                    ahead = not (last and g == GROUPS_B - 1)
                    if c in ACT_CHUNKS:
                        scale_chunk(n, tile, c)
                    if sg == 5 and ahead:
                        x0t_out(n, g + 1, filled(n, (0, 2, 3, 4)[g]))
                    for k in range(PAIR_K):
                        if sg == high_slot(k) and ahead:
                            pair_high(n, g + 1, k)
                    if sg in DIAG_SLOTS and ahead:
                        diagonal(n, g + 1, DIAG_SLOTS.index(sg))
                    if sg == mm_slot(PAIR_K - 1) + 1 and ahead:
                        x1_high(n, g + 1)
                    if last:
                        for step in top_steps(slot - 1):
                            top_out(step)
                    if c == 4 and not (first and tile < LAG):
                        p_out(n, tile - LAG, first)
                    if not first and slot == Z_FIRST:
                        z_out(n, 0, (T16, 0))
                    if not first and slot == Z_FIRST + Z_SLOTS - 1:
                        z_out(n, 1, None, filled(n, 1))

            start = Count(act, 0)
            x0t_out(start, 0, (0, 1))
            for k in range(PAIR_K):
                pair_high(start, 0, k)
                diagonal(start, 0, k)
            diagonal(start, 0, PAIR_K)
            x1_high(start, 0)
            act.wait_ge(s_late, 16 * 8)
            body(0)
            with act.Fori(1, BLOCKS - 1) as b:
                body(b)
            body(BLOCKS - 1, last=True)
            end = Count(act, BLOCKS)
            p_out(end, -2, True)
            for step in range(TOP_EARLY, TOP_ALONE):
                top_out(step)
            p_out(end, -1, True)
            z_out(end, 0, (T16, 0))
            act.wait_ge(s_sh, 5 * BLOCKS)
            act.activation(z[:, 1, BATCH - PART:BATCH], sh_ps[:, 0:PART], ACT.Identity,
                           bias=b2_16[:, :]).then_inc(s_shfree, 1)
            for step in range(TOP_ALONE, len(TOP_ORDER)):
                top_out(step)

        @block.tensor
        def _(pe):
            def chunk(n, tile, c):
                g, t = divmod(tile, TILES_G)
                seq = CHUNKS * tile + c
                if c == 0 and t == 0:
                    n.wait(s_xlo, G4, g + 1)
                back_tile, back_c = divmod(seq - BANKS, CHUNKS)
                if back_c in ACT_CHUNKS:
                    n.wait(s_act, ACT_C * T16, ACT_C * back_tile + act_steps(back_c))
                else:
                    n.wait(s_acc, DVE_FIELDS * T16, DVE_FIELDS * back_tile + dve_steps(back_c))
                cols = slice(c * PER * MAPS, (c * PER + width(c)) * MAPS)
                dst = t_ps[:, seq % BANKS, 0:width(c) * MAPS]
                hi, lo = (x[g % 2][:, t * PART:(t + 1) * PART] for x in (x1_hi, x1_lo))
                pe.matmul(dst, hi, w1_hi[:, cols], start=True, stop=False)
                pe.matmul(dst, hi, w1_lo[:, cols], start=False, stop=False)
                pe.matmul(dst, lo, w1_hi[:, cols], start=False, stop=True).then_inc(s_t, 1)

            def layer0(n, g, k):
                n.wait(s_plo, 7 * G4, 7 * g + k + 1)
                if k == 0:
                    n.wait(s_xlo, G4, g)
                hi, lo = (x[:, k * MAPS:(k + 1) * MAPS] for x in (w0_hi, w0_lo))
                half = (7 * g + k) % 2
                pe.matmul(x1_ps[:, :], hi, pair_hi[:, half, :], start=(k == 0), stop=False)
                pe.matmul(x1_ps[:, :], hi, pair_lo[:, half, :], start=False, stop=False)
                pe.matmul(x1_ps[:, :], lo, pair_hi[:, half, :], start=False,
                          stop=(k == PAIR_K - 1)).then_inc(s_mm0, 1)

            def turn_x0(n, g):
                if isinstance(n.block, int) and n.block == g == 0:
                    pe.wait_ge(s_first, 96)
                else:
                    n.wait(s_load[g % 2], 96 * 2, 96 * (g // 2 + 1))
                for t in range(TILES_G):
                    ins = pe.transpose(sh_ps[:, t * PART:t * PART + ROWS], x0_rep[g % 2][:, t * PART:(t + 1) * PART],
                                       ident_sb[0:ROWS, 0:ROWS])
                ins.then_inc(s_sh, 1)

            def products(n, tile):
                n.wait(s_x2, T16, tile + 1)
                if tile % TILES_G == 0:
                    n.wait(s_diag, BATCH_T * G4, BATCH_T * (tile // TILES_G + 1))
                n.wait(s_pe, T16, tile)
                g, t = divmod(tile, TILES_G)
                pe.matmul(p_ps[:, 0:COLS * BATCH_T], x2_t[:, t, :],
                          x0_diag[:, g % 2, t, :, :].rearrange("p i b -> p (i b)"), start=True, stop=True).then_inc(s_p, 1)

            def layer2(fields):
                for i in fields:
                    ins = pe.matmul(sh_ps[:, 0:PART], w2_sb[:, i, :], p_sb[:, i, :], start=(i == 0),
                                    stop=(i == FIELDS - 1))
                if i == FIELDS - 1:
                    ins.then_inc(s_sh, 1)

            def bank_free(n, x0t, z2_read):
                n.wait(s_x0t, G4, x0t)
                if z2_read:
                    n.wait(s_shfree, 1, 0)

            def body(b, last=False):
                n = Count(pe, b)
                first = isinstance(b, int) and b == 0
                for slot in range(TILES_B * CHUNKS):
                    tile, c = divmod(slot, CHUNKS)
                    g, sg = divmod(slot, SLOTS_G)
                    ahead = not (last and g == GROUPS_B - 1)
                    chunk(n, tile, c)
                    if ahead:
                        if sg == 4:
                            bank_free(n, g + 1, z2_read=g > 0)
                            turn_x0(n, g + 1)
                        for k in range(PAIR_K):
                            if sg == mm_slot(k):
                                layer0(n, g + 1, k)
                    if c == 2 and not (first and tile < LAG):
                        products(n, tile - LAG)
                    if not first and Z_FIRST <= slot < Z_FIRST + Z_SLOTS:
                        if slot == Z_FIRST:
                            n.wait(s_pe, T16, 0)
                            bank_free(n, 2, z2_read=False)
                        k = Z_PER * (slot - Z_FIRST)
                        layer2(range(k, min(k + Z_PER, FIELDS)))
                    if last:
                        if slot == TOP_SLOT:
                            pe.wait_ge(s_plo, 7 * G4 * BLOCKS)
                            pe.wait_ge(s_xlo, G4 * BLOCKS)
                            pe.wait_ge(s_z1, BLOCKS - 1)
                            pe.wait_ge(s_shfree, BLOCKS - 1)
                        for step in top_steps(slot):
                            top(step)

            def top(step):
                piece, m = TOP_ORDER[step]
                a, e = TOP_PIECES[piece]
                w = e - a
                dst = (pair_ps, x1_ps)[step % 2]
                if step >= 2:
                    pe.wait_ge(s_hid, step - 1)
                if m < 4:
                    mc = slice(m * PART, (m + 1) * PART)
                    pe.matmul(dst[:, 0:w], wt1_sb[:, 0, mc], z[:, 0, a:e], start=True, stop=False)
                    pe.matmul(dst[:, 0:w], wt1_sb[:, 1, mc], z[:, 1, a:e], start=False, stop=False)
                    ins = pe.matmul(dst[:, 0:w], wt1_ctx[:, mc], dense_sb[:, a:e], start=False, stop=True)
                elif m < 6:
                    mc = slice((m - 4) * PART, (m - 3) * PART)
                    pe.wait_ge(s_hid, TOP_ORDER.index((piece, 3)) + 1)
                    for k in range(4):
                        ins = pe.matmul(dst[:, 0:w], wt2_sb[:, k, mc], hid1[:, piece % 2, k, 0:w], start=(k == 0), stop=(k == 3))
                else:
                    pe.wait_ge(s_hid, TOP_ORDER.index((piece, 5)) + 1)
                    for k in range(2):
                        ins = pe.matmul(dst[0:1, 0:w], wt3_sb[:, k:k + 1], hid2[:, k, 0:w], start=(k == 0), stop=(k == 1))
                ins.then_inc(s_top, 1)

            start = Count(pe, 0)
            pe.wait_ge(s_const, 16 * 6)
            turn_x0(start, 0)
            pe.wait_ge(s_w0lo, 1)
            for k in range(PAIR_K):
                layer0(start, 0, k)
            pe.wait_ge(s_wlo, CHUNKS)
            body(0)
            pe.wait_ge(s_late, 16 * 8)
            with pe.Fori(1, BLOCKS - 1) as b:
                body(b)
            body(BLOCKS - 1, last=True)
            end = Count(pe, BLOCKS)
            products(end, -2)
            for step in range(TOP_EARLY, TOP_ALONE):
                top(step)
            products(end, -1)
            end.wait(s_pe, T16, 0)
            pe.wait_ge(s_shfree, BLOCKS - 1)
            pe.wait_ge(s_x0t, G4 * BLOCKS)
            layer2(range(FIELDS))
            pe.wait_ge(s_z1, BLOCKS)
            pe.wait_ge(s_shfree, BLOCKS)
            for step in range(TOP_ALONE, len(TOP_ORDER)):
                top(step)

        @block.vector
        def _(dve):
            def pair_product(n, g, k):
                start = isinstance(n.block, int) and n.block == g == 0
                if k == 0 and start:
                    dve.wait_ge(s_first, 96)
                elif k == 1 and start:
                    dve.wait_ge(s_second, 48)
                elif k == (3 if start else 0):
                    n.wait(s_load[g % 2], 96 * 2, 96 * (g // 2 + 1))
                bank, turns = pair_bank(n, g, k)
                n.wait(s_plo, 7 * G4, 7 * g + k + 1 - turns)
                dve.tensor_tensor(bank, x0_rep[g % 2][:, :], x0_shift[g % 2][:, k, :],
                                  ALU.mult).then_inc(s_pair, 1)

            def pair_low(n, g, k):
                n.wait(s_phi, 7 * G4, 7 * g + k + 1)
                half = (7 * g + k) % 2
                dve.tensor_tensor(pair_lo[:, half, :], pair_bank(n, g, k)[0], pair_hi[:, half, :].bitcast(fp32),
                                  ALU.subtract).then_inc(s_plo, 1)

            def x1_low(n, g):
                n.wait(s_xhi, G4, g + 1)
                dve.scalar_tensor_tensor(out=x1_lo[g % 2][:, :], in0=x1_ps[:, :], scalar=b0_col[:, :],
                                         in1=x1_hi[g % 2][:, :].bitcast(fp32), op0=ALU.add,
                                         op1=ALU.subtract).then_inc(s_xlo, 1)

            def add_chunk(n, tile, c):
                g, t = divmod(tile, TILES_G)
                n.wait(s_t, CHUNKS * T16, CHUNKS * tile + c + 1)
                if dve_steps(c) == width(c):
                    if t == 0:
                        n.wait(s_x0t, G4, g + 1)
                    n.wait(s_act, ACT_C * T16, ACT_C * tile + 1)
                for w in range(width(c)):
                    step = dve_steps(c) - width(c) + w
                    acc = dve_part[:, tile % 2, step % 2, :]
                    src = t_ps[:, (CHUNKS * tile + c) % BANKS, w * MAPS:(w + 1) * MAPS]
                    x0 = x0_t[:, g % 2, t, PER * c + w:PER * c + w + 1]
                    if step == 0:
                        ins = dve.scalar_tensor_tensor(out=acc, in0=src, scalar=x0, in1=b1_row[:, :],
                                                       op0=ALU.mult, op1=ALU.add)
                    elif step == 1:
                        ins = dve.scalar_tensor_tensor(out=acc, in0=src, scalar=x0, in1=act_part[:, tile % 2, 0, :],
                                                       op0=ALU.mult, op1=ALU.add)
                    else:
                        n.wait(s_acc, DVE_FIELDS * T16, DVE_FIELDS * tile + step - 1)
                        ins = dve.scalar_tensor_tensor(out=acc, in0=src, scalar=x0, in1=acc,
                                                       op0=ALU.mult, op1=ALU.add)
                    ins.then_inc(s_acc, 1)

            def fold(n, tile):
                n.wait(s_act, ACT_C * T16, ACT_C * tile + 3)
                u = act_part[:, tile % 2, :, :]
                dve.tensor_tensor(u[:, 4:8, :], u[:, 4:8, :], u[:, 8:12, :], ALU.add).then_inc(s_fold, 1)

            def join(n, tile):
                n.wait(s_acc, DVE_FIELDS * T16, DVE_FIELDS * (tile + 1))
                dve.tensor_tensor(act_part[:, tile % 2, 0, :], dve_part[:, tile % 2, 0, :],
                                  dve_part[:, tile % 2, 1, :], ALU.add).then_inc(s_join, 1)

            def body(b, last=False):
                n = Count(dve, b)
                first = isinstance(b, int) and b == 0
                for slot in range(TILES_B * CHUNKS):
                    tile, c = divmod(slot, CHUNKS)
                    g, sg = divmod(slot, SLOTS_G)
                    ahead = not (last and g == GROUPS_B - 1)
                    if c not in ACT_CHUNKS:
                        add_chunk(n, tile, c)
                    if c == FOLD_C:
                        fold(n, tile)
                    if c == 0 and not (first and tile == 0):
                        join(n, tile - 1)
                    if ahead:
                        for k in range(PAIR_K):
                            if sg == pair_slot(k):
                                pair_product(n, g + 1, k)
                            if sg == low_slot(k):
                                pair_low(n, g + 1, k)
                        if sg == mm_slot(PAIR_K - 1) + 2:
                            x1_low(n, g + 1)

            dve.memset(x0_t[:, :, :, FIELDS:COLS], 1.0).then_inc(s_set, 1)
            dve.wait_ge(s_const, 16 * 6)
            dve.tensor_tensor(w0_sum, w0_raw[:, 0, :], w0_raw[:, 1, :],
                              ALU.add).then_inc(s_set, 1)
            dve.wait_ge(s_w0hi, 1)
            dve.tensor_tensor(w0_lo[:, :], w0_sum, w0_hi[:, :].bitcast(fp32), ALU.subtract).then_inc(s_w0lo, 1)
            for c in range(CHUNKS):
                a, e = c * PER * MAPS, min((c + 1) * PER, FIELDS) * MAPS
                dve.wait_ge(s_whi, c + 1)
                dve.tensor_tensor(w1_lo[:, a:e], w1_raw[:, a:e], w1_hi[:, a:e].bitcast(fp32),
                                  ALU.subtract).then_inc(s_wlo, 1)
            start = Count(dve, 0)
            pair_product(start, 0, 0)
            for k in range(PAIR_K):
                if k < PAIR_K - 1:
                    pair_product(start, 0, k + 1)
                pair_low(start, 0, k)
            x1_low(start, 0)
            body(0)
            with dve.Fori(1, BLOCKS - 1) as b:
                body(b)
            body(BLOCKS - 1, last=True)
            join(Count(dve, BLOCKS), -1)


def kernel(**inputs):
    import numpy as np
    import concourse.bacc as bacc
    from concourse.bass_utils import run_bass_kernel_spmd

    nc = bacc.Bacc("TRN2", target_bir_lowering=False, num_devices=1)
    arrays = {}

    def dram(name, a):
        a = np.ascontiguousarray(a)
        arrays[name] = a
        return nc.dram_tensor(name, a.shape, mybir.dt.from_np(a.dtype), kind="ExternalInput").ap()

    field = np.arange(FIELDS)
    first = [field for _ in range(DELTAS)]
    second = [(field + delta) % FIELDS for delta in range(DELTAS)]
    mask = np.repeat(np.eye(BATCH_T, dtype=np.float32), DIM, axis=0)
    w0 = np.asarray(inputs["L0_rec_w0"]).reshape(FIELDS, FIELDS, MAPS)
    i, j = np.stack(first), np.stack(second)
    w0ab = np.zeros((2, PAIR_K * SHIFTS, FIELDS, MAPS), np.float32)
    w0ab[0, :DELTAS] = w0[i, j]
    w0ab[1, 1:DELTAS] = w0[j[1:], i[1:]]
    w0ab = w0ab.reshape(2, PAIR_K, ROWS, MAPS).transpose(2, 0, 1, 3).reshape(ROWS, 2, PAIR_K * MAPS)

    args = [dram("ids", np.asarray(inputs["ids"])),
            [dram(f"tbl_{f}", np.asarray(inputs[f"tbl_{f}"])) for f in range(FIELDS)],
            dram("dense_t", np.asarray(inputs["dense_ctx"]).T),
            dram("mask", mask), dram("ident", np.eye(PART, dtype=np.float32)), dram("w0ab", w0ab)]
    for name in ("L0_rec_b0", "L0_rec_w1", "L0_rec_b1", "L0_rec_w2", "L0_rec_b2", "W_top1", "b_top1", "W_top2",
                 "b_top2", "W_top3"):
        a = np.asarray(inputs[name])
        if name in ("b_top1", "b_top2", "W_top3"):
            a = a.reshape(-1, PART).T
        args.append(dram(name, a))
    out = nc.dram_tensor("out_0", (BATCH, 1), mybir.dt.float32, kind="ExternalOutput").ap()
    cin_kernel(nc, *args, out)
    r = run_bass_kernel_spmd(nc, [arrays], core_ids=[0])
    return r.results[0]["out_0"]
```
